# Optimizing a Trainium2 kernel written in Bass

```python
import numpy as np
import jax
import jax.numpy as jnp

def _softmax(x, axis=-1):
    return jax.nn.softmax(x, axis=axis)

def _gelu(x):
    return jax.nn.gelu(x, approximate=True)

def _silu(x):
    return jax.nn.silu(x)

def _sigmoid(x):
    return jax.nn.sigmoid(x)

def _layernorm(x, axis=-1, eps=1e-05):
    m = jnp.mean(x, axis=axis, keepdims=True)
    v = jnp.var(x, axis=axis, keepdims=True)
    return (x - m) / jnp.sqrt(v + eps)

def _scatter_add(tgt, idx, src, axis=0):
    return tgt.at[idx].add(src)

def _segment_sum(src, seg, n):
    return jax.ops.segment_sum(src, seg, n)
kernel_name = 'mk_macaron_d1_jaxref_r8_170949'

def setup_inputs(seed: int=0):
    np.random.seed(seed)
    _w = jnp.asarray

    def _L0_attn_setup():
        import jax, jax.numpy as jnp
        import numpy as np
        DIM = 256
        HEADS = 16
        HEAD_DIM = DIM // HEADS
        RANK = 16
        ALPHA = 8.0
        SCALING = ALPHA / RANK
        SCALE = HEAD_DIM ** (-0.5)

        def lora_linear(x, W, b, Bm, Am):
            out = jnp.einsum('bld,od->blo', x, W) + b
            upd = jnp.einsum('blr,or->blo', jnp.einsum('bld,rd->blr', x, Bm), Am)
            return out + SCALING * upd

        def _split(t):
            B, L, D = t.shape
            return t.reshape(B, L, HEADS, HEAD_DIM).transpose(0, 2, 1, 3)
        key = jax.random.key(seed)
        ks = jax.random.split(key, 20)
        B, L = (4, 256)
        x = jax.random.normal(ks[0], (B, L, DIM), dtype=jnp.float32)
        s = 0.02
        inp = {'x': x}
        for i, name in enumerate(['q', 'k', 'v', 'o']):
            inp[f'W{name}'] = jax.random.normal(ks[1 + 4 * i], (DIM, DIM), jnp.float32) * s
            inp[f'b{name}'] = jax.random.normal(ks[2 + 4 * i], (DIM,), jnp.float32) * s
            inp[f'B{name}'] = jax.random.normal(ks[3 + 4 * i], (RANK, DIM), jnp.float32) * s
            inp[f'A{name}'] = jax.random.uniform(ks[4 + 4 * i], (DIM, RANK), jnp.float32, -0.1, 0.1)
        return inp
    _L0_attn_in = _L0_attn_setup()

    def _L0_ffn_setup():
        import jax, jax.numpy as jnp
        import numpy as np
        HIDDEN = 256
        INTER = 1024
        RETRIEVAL = 128
        NUM_EXPERTS = 512
        NUM_KEYS = 64
        TOP_K = 8
        B, S = (4, 256)
        key = jax.random.key(seed)
        ks = jax.random.split(key, 8)
        sc = 0.02
        return {'hidden_states': jax.random.normal(ks[0], (B, S, HIDDEN), jnp.float32), 'W_q': jax.random.normal(ks[1], (HIDDEN, RETRIEVAL), jnp.float32) * sc, 'keys': jax.random.normal(ks[2], (2, RETRIEVAL // 2, NUM_KEYS), jnp.float32) * sc, 'down_embed': jax.random.normal(ks[3], (NUM_EXPERTS, HIDDEN), jnp.float32) * sc, 'up_embed': jax.random.normal(ks[4], (NUM_EXPERTS, HIDDEN), jnp.float32) * sc, 'gate_w': jax.random.normal(ks[5], (HIDDEN, INTER), jnp.float32) * sc, 'up_w': jax.random.normal(ks[6], (HIDDEN, INTER), jnp.float32) * sc, 'down_w': jax.random.normal(ks[7], (INTER, HIDDEN), jnp.float32) * sc}
    _L0_ffn_in = _L0_ffn_setup()
    _d = {'L0_attn_x': _L0_attn_in['x'], 'L0_attn_Wq': _L0_attn_in['Wq'], 'L0_attn_bq': _L0_attn_in['bq'], 'L0_attn_Bq': _L0_attn_in['Bq'], 'L0_attn_Aq': _L0_attn_in['Aq'], 'L0_attn_Wk': _L0_attn_in['Wk'], 'L0_attn_bk': _L0_attn_in['bk'], 'L0_attn_Bk': _L0_attn_in['Bk'], 'L0_attn_Ak': _L0_attn_in['Ak'], 'L0_attn_Wv': _L0_attn_in['Wv'], 'L0_attn_bv': _L0_attn_in['bv'], 'L0_attn_Bv': _L0_attn_in['Bv'], 'L0_attn_Av': _L0_attn_in['Av'], 'L0_attn_Wo': _L0_attn_in['Wo'], 'L0_attn_bo': _L0_attn_in['bo'], 'L0_attn_Bo': _L0_attn_in['Bo'], 'L0_attn_Ao': _L0_attn_in['Ao'], 'L0_ffn_W_q': _L0_ffn_in['W_q'], 'L0_ffn_keys': _L0_ffn_in['keys'], 'L0_ffn_down_embed': _L0_ffn_in['down_embed'], 'L0_ffn_up_embed': _L0_ffn_in['up_embed'], 'L0_ffn_gate_w': _L0_ffn_in['gate_w'], 'L0_ffn_up_w': _L0_ffn_in['up_w'], 'L0_ffn_down_w': _L0_ffn_in['down_w']}
    _x0 = _d['L0_attn_x']
    _d['L0_attn_x'] = jax.random.normal(jax.random.fold_in(jax.random.key(seed), 1), (2, 1024, 256), dtype=_x0.dtype)
    del _x0
    return _d

def reference(L0_attn_x, L0_attn_Wq, L0_attn_bq, L0_attn_Bq, L0_attn_Aq, L0_attn_Wk, L0_attn_bk, L0_attn_Bk, L0_attn_Ak, L0_attn_Wv, L0_attn_bv, L0_attn_Bv, L0_attn_Av, L0_attn_Wo, L0_attn_bo, L0_attn_Bo, L0_attn_Ao, L0_ffn_W_q, L0_ffn_keys, L0_ffn_down_embed, L0_ffn_up_embed, L0_ffn_gate_w, L0_ffn_up_w, L0_ffn_down_w):

    def _L0_attn_ref(x, Wq, bq, Bq, Aq, Wk, bk, Bk, Ak, Wv, bv, Bv, Av, Wo, bo, Bo, Ao):
        import jax, jax.numpy as jnp
        import numpy as np
        DIM = 256
        HEADS = 16
        HEAD_DIM = DIM // HEADS
        RANK = 16
        ALPHA = 8.0
        SCALING = ALPHA / RANK
        SCALE = HEAD_DIM ** (-0.5)

        def lora_linear(x, W, b, Bm, Am):
            out = jnp.einsum('bld,od->blo', x, W) + b
            upd = jnp.einsum('blr,or->blo', jnp.einsum('bld,rd->blr', x, Bm), Am)
            return out + SCALING * upd

        def _split(t):
            B, L, D = t.shape
            return t.reshape(B, L, HEADS, HEAD_DIM).transpose(0, 2, 1, 3)
        q = _split(lora_linear(x, Wq, bq, Bq, Aq))
        k = _split(lora_linear(x, Wk, bk, Bk, Ak))
        v = _split(lora_linear(x, Wv, bv, Bv, Av))
        scores = jnp.einsum('bhqd,bhkd->bhqk', q, k) * SCALE
        attn = jax.nn.softmax(scores, axis=-1)
        out = jnp.einsum('bhqk,bhkd->bhqd', attn, v)
        B, H, L, hd = out.shape
        out = out.transpose(0, 2, 1, 3).reshape(B, L, H * hd)
        return lora_linear(out, Wo, bo, Bo, Ao)

    def _L0_ffn_ref(hidden_states, W_q, keys, down_embed, up_embed, gate_w, up_w, down_w):
        import jax, jax.numpy as jnp
        import numpy as np
        HIDDEN = 256
        INTER = 1024
        RETRIEVAL = 128
        NUM_EXPERTS = 512
        NUM_KEYS = 64
        TOP_K = 8
        B, S = (4, 256)
        b, s, h = hidden_states.shape
        n = b * s
        queries = (hidden_states @ W_q).reshape(2, n, RETRIEVAL // 2)
        routing = jnp.einsum('tnd,tdk->tnk', queries, keys)
        scores2, idx2 = jax.lax.top_k(routing, TOP_K)
        sx, sy = (scores2[0], scores2[1])
        ix, iy = (idx2[0], idx2[1])
        all_scores = (sx[:, :, None] + sy[:, None, :]).reshape(n, TOP_K * TOP_K)
        all_idx = (ix[:, :, None] * NUM_KEYS + iy[:, None, :]).reshape(n, TOP_K * TOP_K)
        scores, pk = jax.lax.top_k(all_scores, TOP_K)
        indices = jnp.take_along_axis(all_idx, pk, axis=-1)
        de = down_embed[indices]
        ue = up_embed[indices]
        x = hidden_states.reshape(n, h)
        ew = jnp.einsum('nh,nkh->nk', x, de)
        ew = jax.nn.silu(ew) * jax.nn.softmax(scores, axis=-1)
        experts_states = jnp.einsum('nk,nkh->nh', ew, ue).reshape(b, s, h)
        mlp = jax.nn.silu(x @ gate_w) * (x @ up_w) @ down_w
        return mlp.reshape(b, s, h) + experts_states
    x = L0_attn_x
    x = x + 0.5 * _L0_ffn_ref(_layernorm(x, axis=-1), L0_ffn_W_q, L0_ffn_keys, L0_ffn_down_embed, L0_ffn_up_embed, L0_ffn_gate_w, L0_ffn_up_w, L0_ffn_down_w)
    x = x + _L0_attn_ref(_layernorm(x, axis=-1), L0_attn_Wq, L0_attn_bq, L0_attn_Bq, L0_attn_Aq, L0_attn_Wk, L0_attn_bk, L0_attn_Bk, L0_attn_Ak, L0_attn_Wv, L0_attn_bv, L0_attn_Bv, L0_attn_Av, L0_attn_Wo, L0_attn_bo, L0_attn_Bo, L0_attn_Ao)
    x = x + 0.5 * _L0_ffn_ref(_layernorm(x, axis=-1), L0_ffn_W_q, L0_ffn_keys, L0_ffn_down_embed, L0_ffn_up_embed, L0_ffn_gate_w, L0_ffn_up_w, L0_ffn_down_w)
    return x

_drawn_inputs = setup_inputs


def setup_inputs(seed=0):
    import zlib

    import numpy as np

    out = dict(_drawn_inputs(seed))
    spreads = {}
    factors = {'L0_attn_Wq': 8.0,
     'L0_attn_bq': 8.0,
     'L0_attn_Bq': 8.0,
     'L0_attn_Aq': 8.0,
     'L0_attn_Wk': 8.0,
     'L0_attn_bk': 64.0,
     'L0_attn_Bk': 8.0,
     'L0_attn_Ak': 8.0,
     'L0_attn_Wv': 8.0,
     'L0_attn_bv': 8.0,
     'L0_attn_Bv': 8.0,
     'L0_attn_Av': 8.0,
     'L0_attn_Wo': 8.0,
     'L0_attn_bo': 23.312,
     'L0_attn_Bo': 8.0,
     'L0_attn_Ao': 8.0,
     'L0_ffn_W_q': 8.0,
     'L0_ffn_keys': 8.0,
     'L0_ffn_down_embed': 8.0,
     'L0_ffn_up_embed': 8.0}
    for name, (base, spread) in spreads.items():
        noise = np.random.default_rng([zlib.crc32(name.encode()), seed]).standard_normal(out[name].shape)
        drawn = base * np.exp(spread * noise) if base else spread * noise
        out[name] = jnp.asarray(drawn.astype(out[name].dtype))
    for name, factor in factors.items():
        out[name] = (out[name] * factor).astype(out[name].dtype)
    return out
```

```python
from contextlib import ExitStack

import concourse.bass as bass
from concourse import mybir

F32 = mybir.dt.float32
F32R = mybir.dt.float32r
ALU = mybir.AluOpType
ACT = mybir.ActivationFunctionType
AXIS_X = mybir.AxisListType.X
ds = bass.ds

P = 128
BATCH, SEQ, DIM = 2, 1024, 256
TOKENS = BATCH * SEQ
KT = DIM // P
TILES = TOKENS // P
JT = SEQ // P
CHUNK = 512
CHUNKS = TOKENS // CHUNK
CT = CHUNK // P
HEADS, HD, RANK = 16, 16, 16
LORA_SCALE = 8.0 / RANK
SCORE_SCALE = HD ** -0.5
INTER, EXPERTS, KEYS, RETRIEVAL, TOP = 1024, 512, 64, 128, 8
GRID_ROWS = EXPERTS // KEYS
FT = INTER // P
ET = EXPERTS // P
UNITS = FT + ET
EPS = 1e-5
FIRST = 2


def product3(pe, out, w, x):
    last = len(w) - 1
    for k, ((w_hi, w_lo), (x_hi, x_lo)) in enumerate(zip(w, x)):
        pe.matmul(out, w_hi, x_hi, start=(k == 0), stop=False)
        pe.matmul(out, w_lo, x_hi, start=False, stop=False)
        done = pe.matmul(out, w_hi, x_lo, start=False, stop=(k == last))
    return done


class Norm:

    def __init__(self, name, sb, psum, sem, halves, rows_width):
        self.xhi, self.xlo = halves
        self.stats = sb(f"{name}_stats", [P, TILES, 6], F32)
        self.work = sb(f"{name}_work", [P, 4, TILES], F32)
        self.mean = sb(f"{name}_mean", [P, TILES], F32)
        self.var = sb(f"{name}_var", [P, TILES], F32)
        self.rstd = sb(f"{name}_rstd", [P, TILES], F32)
        self.xn = sb(f"{name}_xn", [P, 2, BATCH, DIM], F32)
        self.full = sb(f"{name}_full", [P, 2, KT, BATCH, P], F32)
        self.turned_ps = psum(f"{name}_turned", [P, 2, KT, BATCH, P], F32)
        self.rows_ps = psum(f"{name}_rows", [P, 2, 512], F32)
        self.rows_width = rows_width
        self.stats_done = sem(f"{name}_stats_done")
        self.var_done = sem(f"{name}_var_done")
        self.rstd_done = sem(f"{name}_rstd_done")
        self.xn_done = sem(f"{name}_xn_done")
        self.turned = sem(f"{name}_turned_done")
        self.full_done = sem(f"{name}_full_done")
        self.hi_done = sem(f"{name}_hi_done")
        self.lo_done = sem(f"{name}_lo_done")
        self.rows_done = sem(f"{name}_rows_done")
        self.rows_out = sem(f"{name}_rows_out")

    def token_halves(self, c):
        hi = self.xhi[:, :, :, :].rearrange("p k b s -> p k (b s)")
        lo = self.xlo[:, :, :, :].rearrange("p k b s -> p k (b s)")
        return [(hi[:, k, ds(c * CHUNK, CHUNK)], lo[:, k, ds(c * CHUNK, CHUNK)]) for k in range(KT)]


def norm_on_vector(v, n, x_sb, rows_evacuation=None):
    with v.Fori(0, TILES) as t:
        v.bn_stats(n.stats[:, t, :], x_sb[:, t, :]).then_inc(n.stats_done, 1)
    v.wait_ge(n.stats_done, TILES)
    even_mean, odd_mean = n.stats[:, :, 1], n.stats[:, :, 4]
    even_m2, odd_m2 = n.stats[:, :, 2], n.stats[:, :, 5]
    v.tensor_tensor(n.work[:, 0, :], even_mean, odd_mean, ALU.add).then_inc(n.var_done, 1)
    v.tensor_tensor(n.work[:, 1, :], even_mean, odd_mean, ALU.subtract).then_inc(n.var_done, 1)
    v.tensor_tensor(n.work[:, 2, :], even_m2, odd_m2, ALU.add).then_inc(n.var_done, 1)
    v.wait_ge(n.var_done, 3)
    v.tensor_scalar(n.mean[:, :], n.work[:, 0, :], 0.5, None, ALU.mult).then_inc(n.var_done, 1)
    v.tensor_tensor(n.work[:, 3, :], n.work[:, 1, :], n.work[:, 1, :], ALU.mult).then_inc(n.var_done, 1)
    v.wait_ge(n.var_done, 5)
    v.tensor_scalar(n.work[:, 0, :], n.work[:, 3, :], 0.25, EPS, ALU.mult, ALU.add).then_inc(n.var_done, 1)
    v.wait_ge(n.var_done, 6)
    v.scalar_tensor_tensor(out=n.var[:, :], in0=n.work[:, 2, :], scalar=1.0 / DIM, in1=n.work[:, 0, :],
                           op0=ALU.mult, op1=ALU.add).then_inc(n.var_done, 1)
    v.wait_ge(n.rstd_done, 1)
    with v.Fori(0, JT // 2) as pair:
        j0 = pair * 2
        for par in range(2):
            v.wait_ge(n.turned, j0 + par + 1)
            for b in range(BATCH):
                t = b * JT + j0 + par
                v.tensor_scalar(n.xn[:, par, b, :], x_sb[:, t, :], n.mean[:, ds(t, 1)], n.rstd[:, ds(t, 1)],
                                ALU.subtract, ALU.mult).then_inc(n.xn_done, 1)
        for par in range(2):
            at = ds((j0 + par) * P, P)
            v.wait_ge(n.hi_done, j0 + par + 1)
            v.tensor_tensor(n.xlo[:, :, :, at], n.turned_ps[:, par, :, :, :], n.xhi[:, :, :, at].bitcast(F32),
                            ALU.subtract).then_inc(n.lo_done, 1)
        if rows_evacuation is not None:
            for par in range(2):
                v.wait_ge(n.rows_done, j0 + par + 1 + FIRST)
                rows_evacuation(v, j0 + par, par)


def norm_on_gpsimd(pool, n, minus_half):
    pool.wait_ge(n.var_done, 7)
    pool.tensor_tensor(n.rstd[:, :], n.var[:, :], minus_half, ALU.pow).then_inc(n.rstd_done, 1)


def norm_on_tensor(pe, n, ident, rows_weights):
    pe.sem_inc(n.turned, FIRST)
    pe.sem_inc(n.rows_done, FIRST)
    with pe.Fori(0, JT // 2) as pair:
        j0 = pair * 2
        for par in range(2):
            pe.wait_ge(n.xn_done, (j0 + par + 1) * BATCH)
            pe.wait_ge(n.lo_done, j0 + par + 1)
            for k in range(KT):
                for b in range(BATCH):
                    turned = pe.transpose(n.turned_ps[:, par, k, b, :], n.xn[:, par, b, k * P:(k + 1) * P], ident)
            turned.then_inc(n.turned, 1)
        for par in range(2):
            pe.wait_ge(n.full_done, j0 + par + 1)
            pe.wait_ge(n.rows_out, j0 + par + 1)
            w = n.rows_width
            for b in range(BATCH):
                for k in range(KT):
                    rows = pe.matmul(n.rows_ps[:, par, b * w:(b + 1) * w], n.full[:, par, k, b, :],
                                     rows_weights(k, b), start=(k == 0), stop=(k == KT - 1))
            rows.then_inc(n.rows_done, 1)


def norm_on_scalar(act, n, rows_evacuation=None):
    with act.Fori(0, JT // 2) as pair:
        j0 = pair * 2
        for par in range(2):
            act.wait_ge(n.turned, j0 + par + 1 + FIRST)
            act.wait_ge(n.rows_done, j0 + par + 1)
            act.activation(n.full[:, par, :, :, :], n.turned_ps[:, par, :, :, :], ACT.Copy).then_inc(n.full_done, 1)
            act.activation(n.xhi[:, :, :, ds((j0 + par) * P, P)], n.turned_ps[:, par, :, :, :],
                           ACT.Copy).then_inc(n.hi_done, 1)
        if rows_evacuation is not None:
            for par in range(2):
                act.wait_ge(n.rows_done, j0 + par + 1 + FIRST)
                rows_evacuation(act, j0 + par, par)


def setup_block(nc, outer, sem, dram, keep):
    with ExitStack() as scope:
        def sb(name, shape, dt):
            return scope.enter_context(nc.sbuf_tensor(name, shape, dt))

        wq_rows = sb("wq_rows", [RETRIEVAL // 2, 2, DIM], F32)
        keys_sb = sb("keys_sb", [RETRIEVAL // 2, 2, KEYS], F32)
        fold_ps = scope.enter_context(nc.psum_tensor("fold_ps", [P, KT, 2, 2, KEYS], F32))
        wq_in, keys_in = sem("wq_in"), sem("keys_in")
        ident_zero, folded, fold_out = sem("ident_zero"), sem("folded"), sem("fold_out")
        block = scope.enter_context(nc.Block())

        @block.sync
        def _(sp):
            sp.dma_start(wq_rows[:, :, :], dram["retrieval_t"].rearrange("(h d) x -> d h x", h=2)).then_inc(wq_in, 16)
            sp.dma_start(keys_sb[:, :, :], dram["keys"].rearrange("t d k -> d t k")).then_inc(keys_in, 16)
            x_tiles = dram["x"].rearrange("(t p) d -> p t d", p=P)
            for c in range(CHUNKS):
                sp.dma_start(keep["x"][:, c * CT:(c + 1) * CT, :], x_tiles[:, c * CT:(c + 1) * CT, :]
                             ).then_inc(keep["x_in"], 16)

        @block.gpsimd
        def _(pool):
            pool.memset(keep["ident"][:, :], 0.0).then_inc(ident_zero, 1)
            pool.memset(keep["minus_half"][:, :], -0.5).then_inc(keep["ident_done"], 1)
            pool.wait_ge(ident_zero, 1)
            pool.affine_select(out=keep["ident"][:, :], in_=keep["ident"][:, :], compare_op=ALU.not_equal,
                               fill=1.0, base=0, pattern=[[-1, P]], channel_multiplier=1
                               ).then_inc(keep["ident_done"], 1)

        @block.tensor
        def _(pe):
            pe.wait_ge(wq_in, 16)
            pe.wait_ge(keys_in, 16)
            for half in range(2):
                for k in range(KT):
                    for t in range(2):
                        fold = pe.matmul(fold_ps[:, k, t, half, :], wq_rows[:, half, k * P:(k + 1) * P],
                                         keys_sb[:, t, :], start=True, stop=True)
            fold.then_inc(folded, 1)

        @block.vector
        def _(v):
            v.wait_ge(folded, 1)
            v.tensor_copy(keep["route_w"][:, :, :, :, :], fold_ps[:, :, :, :, :]).then_inc(fold_out, 1)


def ffn_block(nc, sem_of, dram, keep, layer):
    first, store = layer == 0, layer == 1
    x_sb, ident = keep["x"], keep["ident"]
    name = f"ffn{layer}"
    with ExitStack() as scope:
        def sb(n, shape, dt):
            return scope.enter_context(nc.sbuf_tensor(f"{name}_{n}", shape, dt))

        def psum(n, shape, dt):
            return scope.enter_context(nc.psum_tensor(f"{name}_{n}", shape, dt))

        def sem(n):
            return sem_of(f"{name}_{n}")

        parts = (("gate", INTER), ("up", INTER), ("down_embed", EXPERTS))
        hi = {w: sb(f"{w}_hi", [P, KT, n], F32R) for w, n in parts}
        lo = {w: sb(f"{w}_lo", [P, KT, n], F32R) for w, n in parts}
        down = sb("down", [P, FT, DIM], F32)
        up_embed = sb("up_embed", [P, ET, DIM], F32)
        routes = sb("routes", [P, JT, 2, 2, KEYS], F32)
        hidden = sb("hidden", [P, UNITS, CHUNK], F32)
        tanh = sb("tanh", [P, 2, CHUNK], F32)
        gated = sb("gated", [P, 2, CHUNK], F32)
        mix = sb("mix", [P, 2, 2, EXPERTS], F32)
        r = sb("r", [P, 2, 2, 2, KEYS], F32)
        best = sb("best", [P, 2, 2, 2, TOP], F32)
        below = sb("below", [P, 2, 2, 2, KEYS], F32)
        expo = sb("expo", [P, 2, 2, 2, KEYS], F32)
        pairs = sb("pairs", [P, 2, 2, TOP, TOP], F32)
        top = sb("top", [P, 2, 2, TOP], F32)
        top_below = sb("top_below", [P, 2, 2, TOP], F32)
        top_exp = sb("top_exp", [P, 2, 2, TOP], F32)
        total = sb("total", [P, 2, 2], F32)
        inverse = sb("inverse", [P, 2, 2], F32)
        row_exp = sb("row_exp", [P, 2, 2, GRID_ROWS], F32)
        sums = sb("sums", [P, 2, 2, GRID_ROWS, KEYS], F32)
        grid = sb("grid", [P, 2, 2, GRID_ROWS, KEYS], F32)
        inside = sb("inside", [P, 2, 2], F32)
        clipped = sb("clipped", [P, 2, 2], F32)

        halves = [sb(f"x{part}", [P, KT, BATCH, SEQ], F32R) for part in ("hi", "lo")]

        part_in = {w: sem(f"{w}_in") for w, _ in parts}
        down_in, up_embed_in = sem("down_in"), sem("up_embed_in")
        part_hi, part_lo = sem("part_hi"), sem("part_lo")
        route_in = sem("route_in")
        scored = sem("scored")
        route_exp = sem("route_exp")
        scaled = sem("scaled")
        grid_done = sem("grid_done")
        mixed = sem("mixed")
        gate_ready, up_ready = sem("gate_ready"), sem("up_ready")
        tanh_done, gated_done, hidden_done = sem("tanh_done"), sem("gated_done"), sem("hidden_done")
        mix_turned, out_ready, x_updated = sem("mix_turned"), sem("out_ready"), sem("x_updated")
        stored = sem("stored")

        with ExitStack() as norm_scope:
            def norm_sb(n, shape, dt):
                return norm_scope.enter_context(nc.sbuf_tensor(n, shape, dt))

            def norm_psum(n, shape, dt):
                return norm_scope.enter_context(nc.psum_tensor(n, shape, dt))

            stage = {w: norm_scope.enter_context(nc.sbuf_tensor(f"{name}_{w}_stage", [P, KT, n], F32))
                     for w, n in parts}
            n = Norm(f"{name}_norm", norm_sb, norm_psum, sem_of, halves, KEYS * 2)
            block = norm_scope.enter_context(nc.Block())

            @block.sync
            def _(sp):
                for w, _ in parts:
                    sp.dma_start(stage[w][:, :, :], dram[w].rearrange("(k p) f -> p k f", p=P)
                                 ).then_inc(part_in[w], 16)
                sp.dma_start(down[:, :, :], dram["down"].rearrange("(f p) d -> p f d", p=P)).then_inc(down_in, 16)
                sp.dma_start(up_embed[:, :, :], dram["up_embed"].rearrange("(f p) d -> p f d", p=P)
                             ).then_inc(up_embed_in, 16)

            @block.gpsimd
            def _(pool):
                norm_on_gpsimd(pool, n, keep["minus_half"][:, :])

            @block.tensor
            def _(pe):
                pe.wait_ge(keep["ident_done"], 2)
                norm_on_tensor(pe, n, ident[:, :],
                               lambda k, b: keep["route_w"][:, k, b, :, :].rearrange("p h k -> p (h k)"))

            @block.scalar
            def _(act):
                act.sem_inc(n.rows_out, FIRST)

                def routes_out(act, j, par):
                    act.activation(routes[:, j, :, :, :],
                                   n.rows_ps[:, par, 0:4 * KEYS].rearrange("p (b h k) -> p b h k", b=2, h=2),
                                   ACT.Copy).then_inc(n.rows_out, 1)

                norm_on_scalar(act, n, routes_out)
                for w, _ in parts:
                    act.wait_ge(part_in[w], 16)
                    act.activation(hi[w][:, :, :], stage[w][:, :, :], ACT.Copy).then_inc(part_hi, 1)

            @block.vector
            def _(v):
                v.sem_inc(n.lo_done, FIRST)
                if first:
                    v.wait_ge(keep["x_in"], 16 * CHUNKS)
                norm_on_vector(v, n, x_sb)
                for i, (w, _) in enumerate(parts):
                    v.wait_ge(part_hi, i + 1)
                    v.tensor_tensor(lo[w][:, :, :], stage[w][:, :, :], hi[w][:, :, :].bitcast(F32),
                                    ALU.subtract).then_inc(part_lo, 1)

        gate_ps = psum("gate_ps", [P, 2, CHUNK], F32)
        up_ps = psum("up_ps", [P, 2, CHUNK], F32)
        mix_ps = psum("mix_ps", [P, 2, CHUNK], F32)
        out_ps = psum("out_ps", [P, 2, 512], F32)
        block = scope.enter_context(nc.Block())
        SCORE_STEPS, SCALE_STEPS, MIX_STEPS = 11, 3, 4

        def weight(w, i):
            at = slice(i * P, (i + 1) * P)
            return [(hi[w][:, k, at], lo[w][:, k, at]) for k in range(KT)]

        @block.tensor
        def _(pe):
            pe.wait_ge(part_lo, len(parts))
            with pe.Fori(0, CHUNKS) as c:
                tokens = n.token_halves(c)
                for u in range(FT):
                    if u >= 2:
                        pe.wait_ge(hidden_done, c * UNITS + u - 1)
                    product3(pe, gate_ps[:, u % 2, :], weight("gate", u), tokens).then_inc(gate_ready, 1)
                    product3(pe, up_ps[:, u % 2, :], weight("up", u), tokens).then_inc(up_ready, 1)
                def expert_product(e):
                    pe.wait_ge(gated_done, c * UNITS + FT + e - 1)
                    product3(pe, gate_ps[:, e % 2, :], weight("down_embed", e), tokens).then_inc(gate_ready, 1)

                def turn_mix(e):
                    if e >= 2:
                        pe.wait_ge(hidden_done, c * UNITS + FT + e - 1)
                    for jh in range(4):
                        turn = pe.transpose(mix_ps[:, e % 2, jh * P:(jh + 1) * P],
                                            mix[:, jh // 2, jh % 2, e * P:(e + 1) * P], ident[:, :])
                    turn.then_inc(mix_turned, 1)

                expert_product(0)
                expert_product(1)
                pe.wait_ge(mixed, (c + 1) * 2 * MIX_STEPS)
                turn_mix(0)
                turn_mix(1)
                for e in range(2, ET):
                    expert_product(e)
                    turn_mix(e)
                pe.wait_ge(down_in, 16)
                pe.wait_ge(up_embed_in, 16)
                for tt in range(CT):
                    if tt >= 2:
                        pe.wait_ge(x_updated, c * CT + tt - 1)
                    for u in range(UNITS):
                        if tt == 0:
                            pe.wait_ge(hidden_done, c * UNITS + u + 1)
                        rhs = down[:, u, :] if u < FT else up_embed[:, u - FT, :]
                        out = pe.matmul(out_ps[:, tt % 2, 0:DIM], hidden[:, u, tt * P:(tt + 1) * P], rhs,
                                        start=(u == 0), stop=(u == UNITS - 1))
                    out.then_inc(out_ready, 1)

        @block.scalar
        def _(act):
            def fetch_routes(j, jp):
                act.activation(r[:, jp, :, :, :], routes[:, j, :, :, :], ACT.Copy).then_inc(route_in, 1)

            def route_exps(j, jp):
                act.wait_ge(scored, (j + 1) * SCORE_STEPS)
                act.activation(expo[:, jp, :, :, :], below[:, jp, :, :, :], ACT.Exp).then_inc(route_exp, 1)
                act.activation(top_exp[:, jp, :, :], top_below[:, jp, :, :], ACT.Exp).then_inc(route_exp, 1)

            def units(c):
                for u in range(UNITS):
                    act.wait_ge(gate_ready, c * UNITS + u + 1)
                    if u >= 2:
                        act.wait_ge(gated_done, c * UNITS + u - 1)
                    act.activation(tanh[:, u % 2, :], gate_ps[:, u % 2, :], ACT.Tanh, scale=0.5
                                   ).then_inc(tanh_done, 1)

            def route(c):
                for jp in range(2):
                    fetch_routes(c * 2 + jp, jp)
                for jp in range(2):
                    route_exps(c * 2 + jp, jp)

            route(0)
            with act.Fori(0, CHUNKS - 1) as c:
                units(c)
                route(c + 1)
            units(CHUNKS - 1)

        @block.gpsimd
        def _(pool):
            with pool.Fori(0, JT // 2) as pair:
                j0 = pair * 2
                for jp in range(2):
                    pool.wait_ge(scaled, (j0 + jp + 1) * SCALE_STEPS)
                    for h in range(2):
                        row = row_exp[:, jp, h, :].unsqueeze(2).broadcast_to([P, GRID_ROWS, KEYS])
                        col = expo[:, jp, 1, h, :].unsqueeze(1).broadcast_to([P, GRID_ROWS, KEYS])
                        pool.tensor_tensor(grid[:, jp, h, :, :], row, col, ALU.mult).then_inc(grid_done, 1)

        @block.vector
        def _(v):
            def score(j, jp):
                def pair_sums(h):
                    v.tensor_tensor(sums[:, jp, h, :, :],
                                    r[:, jp, 0, h, 0:GRID_ROWS].unsqueeze(2).broadcast_to([P, GRID_ROWS, KEYS]),
                                    r[:, jp, 1, h, :].unsqueeze(1).broadcast_to([P, GRID_ROWS, KEYS]),
                                    ALU.add).then_inc(scored, 1)

                v.wait_ge(route_in, j + 1)
                pair_sums(0)
                for b in range(2):
                    for h in range(2):
                        v.max(best[:, jp, b, h, :], r[:, jp, b, h, :]).then_inc(scored, 1)
                v.wait_ge(scored, j * SCORE_STEPS + 5)
                v.tensor_tensor(pairs[:, jp, :, :, :],
                                best[:, jp, 0, :, :].unsqueeze(3).broadcast_to([P, 2, TOP, TOP]),
                                best[:, jp, 1, :, :].unsqueeze(2).broadcast_to([P, 2, TOP, TOP]),
                                ALU.add).then_inc(scored, 1)
                v.tensor_tensor(below[:, jp, :, :, :].rearrange("p b h k -> p (b h) k"),
                                r[:, jp, :, :, :].rearrange("p b h k -> p (b h) k"),
                                best[:, jp, :, :, 0:1].rearrange("p b h o -> p (b h) o").broadcast_to([P, 4, KEYS]),
                                ALU.subtract).then_inc(scored, 1)
                v.wait_ge(scored, j * SCORE_STEPS + 6)
                pair_sums(1)
                for h in range(2):
                    v.max(top[:, jp, h, :], pairs[:, jp, h, :, :]).then_inc(scored, 1)
                v.wait_ge(scored, j * SCORE_STEPS + 10)
                v.tensor_tensor(top_below[:, jp, :, :], top[:, jp, :, :],
                                top[:, jp, :, 0:1].broadcast_to([P, 2, TOP]), ALU.subtract).then_inc(scored, 1)

            def scale(j, jp):
                v.wait_ge(route_exp, (j + 1) * 2)
                v.reduce_sum(total[:, jp, :], top_exp[:, jp, :, :], axis=AXIS_X).then_inc(scaled, 1)
                v.wait_ge(scaled, j * SCALE_STEPS + 1)
                v.reciprocal(inverse[:, jp, :], total[:, jp, :]).then_inc(scaled, 1)
                v.wait_ge(scaled, j * SCALE_STEPS + 2)
                v.tensor_tensor(row_exp[:, jp, :, :], expo[:, jp, 0, :, 0:GRID_ROWS],
                                inverse[:, jp, :].unsqueeze(2).broadcast_to([P, 2, GRID_ROWS]),
                                ALU.mult).then_inc(scaled, 1)

            def blend(j, jp):
                v.wait_ge(grid_done, (j + 1) * 2)
                v.wait_ge(scored, (j + 1) * SCORE_STEPS)
                for h in range(2):
                    v.scalar_tensor_tensor(out=mix[:, jp, h, :],
                                           in0=sums[:, jp, h, :, :].rearrange("p a b -> p (a b)"),
                                           scalar=top[:, jp, h, TOP - 1:TOP],
                                           in1=grid[:, jp, h, :, :].rearrange("p a b -> p (a b)"),
                                           op0=ALU.is_ge, op1=ALU.mult,
                                           accum_out=inside[:, jp, h:h + 1]).then_inc(mixed, 1)
                v.wait_ge(mixed, j * MIX_STEPS + 2)
                v.tensor_scalar(clipped[:, jp, :], inside[:, jp, :], -1.0, 1.0, ALU.mult, ALU.add).then_inc(mixed, 1)
                v.wait_ge(mixed, j * MIX_STEPS + 3)
                v.tensor_tensor(mix[:, jp, :, EXPERTS - 1], mix[:, jp, :, EXPERTS - 1], clipped[:, jp, :],
                                ALU.add).then_inc(mixed, 1)

            def gate_unit(c, u):
                v.wait_ge(tanh_done, c * UNITS + u + 1)
                v.scalar_tensor_tensor(out=gated[:, u % 2, :], in0=tanh[:, u % 2, :], scalar=1.0,
                                       in1=gate_ps[:, u % 2, :], op0=ALU.add, op1=ALU.mult).then_inc(gated_done, 1)
                v.wait_ge(gated_done, c * UNITS + u + 1)

            def units(c):
                for u in range(FT):
                    gate_unit(c, u)
                    v.wait_ge(up_ready, c * FT + u + 1)
                    v.tensor_tensor(hidden[:, u, :], gated[:, u % 2, :], up_ps[:, u % 2, :],
                                    ALU.mult).then_inc(hidden_done, 1)
                for e in range(ET):
                    gate_unit(c, FT + e)
                    v.wait_ge(mix_turned, c * ET + e + 1)
                    v.tensor_tensor(hidden[:, FT + e, :].rearrange("p (j i h) -> p j i h", j=2, h=2),
                                    gated[:, (FT + e) % 2, :].rearrange("p (j i h) -> p j i h", j=2, h=2),
                                    mix_ps[:, e % 2, :].rearrange("p (j h i) -> p j i h", j=2, h=2),
                                    ALU.mult).then_inc(hidden_done, 1)

            def update(c, tt):
                v.wait_ge(out_ready, c * CT + tt + 1)
                v.scalar_tensor_tensor(out=x_sb[:, c * CT + tt, :], in0=out_ps[:, tt % 2, 0:DIM], scalar=0.25,
                                       in1=x_sb[:, c * CT + tt, :], op0=ALU.mult, op1=ALU.add
                                       ).then_inc(x_updated, 1)

            for step in (score, scale, blend):
                for jp in range(2):
                    step(jp, jp)
            with v.Fori(0, CHUNKS - 1) as c:
                units(c)
                for tt, step in enumerate((score, scale, blend)):
                    if step is blend:
                        v.wait_ge(mix_turned, (c + 1) * ET)
                    for jp in range(2):
                        step((c + 1) * 2 + jp, jp)
                    update(c, tt)
                update(c, CT - 1)
            units(CHUNKS - 1)
            for tt in range(CT):
                update(CHUNKS - 1, tt)

        @block.sync
        def _(sp):
            if store:
                out_tiles = dram["out"].rearrange("(t p) d -> p t d", p=P)
                with sp.Fori(0, CHUNKS) as c:
                    sp.wait_ge(x_updated, (c + 1) * CT)
                    sp.dma_start(out_tiles[:, ds(c * CT, CT), :], x_sb[:, ds(c * CT, CT), :]).then_inc(stored, 16)
                sp.wait_ge(stored, CHUNKS * 16)


def project_block(nc, sem, dram, keep, attn):
    x_sb, ident = keep["x"], keep["ident"]
    with ExitStack() as scope:
        def sb(n, shape, dt):
            return scope.enter_context(nc.sbuf_tensor(f"proj_{n}", shape, dt))

        def psum(n, shape, dt):
            return scope.enter_context(nc.psum_tensor(f"proj_{n}", shape, dt))

        wide = ("q", "k")
        w_hi = {p: sb(f"w{p}_hi", [P, KT, DIM], F32R) for p in wide}
        w_lo = {p: sb(f"w{p}_lo", [P, KT, DIM], F32R) for p in wide}
        w_v = sb("wv", [P, KT, DIM], F32)
        bias_v = sb("bias_v", [P, DIM], F32)
        bias = {p: sb(f"bias_{p}", [P, KT], F32) for p in wide}
        halves = [sb(f"x{part}", [P, KT, BATCH, SEQ], F32R) for part in ("hi", "lo")]
        n = Norm("proj_norm", sb, psum, sem, halves, DIM)
        stage = {p: sb(f"w{p}_stage", [P, KT, DIM], F32) for p in "qkv"}
        whole = {p: sb(f"w{p}_whole", [P, KT, DIM], F32) for p in wide} | {"v": w_v}
        lora_b = {p: sb(f"lora_b{p}", [RANK, DIM], F32) for p in "qkv"}
        lora_a = {p: sb(f"lora_a{p}", [RANK, DIM], F32) for p in "qkv"}
        update_ps = psum("update_ps", [P, 2, KT, DIM], F32)
        qk_ps = psum("qk_ps", [P, 2, CHUNK], F32)

        weights_in = {p: sem(f"proj_w{p}_in") for p in "qkv"}
        bias_in = sem("proj_bias_in")
        update_ready = sem("proj_update_ready")
        whole_done = sem("proj_whole_done")
        w_hi_done, w_lo_done = sem("proj_w_hi_done"), sem("proj_w_lo_done")
        qk_ready = sem("proj_qk_ready")
        qk_hi_done = sem("proj_qk_hi_done")
        qk_lo_done = sem("proj_qk_lo_done")
        block = scope.enter_context(nc.Block())

        @block.sync
        def _(sp):
            for p in "qkv":
                sp.dma_start(stage[p][:, :, :], dram[f"w{p}_t"].rearrange("(k p) o -> p k o", p=P)
                             ).then_inc(weights_in[p], 16)
                sp.dma_start(lora_b[p][:, :], dram[f"lora_b{p}"]).then_inc(weights_in[p], 16)
                sp.dma_start(lora_a[p][:, :], dram[f"lora_a{p}_t"]).then_inc(weights_in[p], 16)
            for p in wide:
                sp.dma_start(bias[p][:, :], dram[f"b{p}_columns"]).then_inc(bias_in, 16)
            sp.dma_start(bias_v[:, :], dram["bv"].partition_broadcast(P)).then_inc(bias_in, 16)

        @block.gpsimd
        def _(pool):
            norm_on_gpsimd(pool, n, keep["minus_half"][:, :])

        @block.tensor
        def _(pe):
            for i, p in enumerate("qkv"):
                pe.wait_ge(weights_in[p], 48)
                if i >= 2:
                    pe.wait_ge(whole_done, i - 1)
                for k in range(KT):
                    update = pe.matmul(update_ps[:, i % 2, k, :], lora_b[p][:, k * P:(k + 1) * P], lora_a[p][:, :],
                                       start=True, stop=True)
                update.then_inc(update_ready, 1)
            pe.wait_ge(whole_done, 3)
            norm_on_tensor(pe, n, ident[:, :], lambda k, b: w_v[:, k, :])
            pe.wait_ge(w_lo_done, len(wide))
            with pe.Fori(0, CHUNKS) as c:
                tokens = n.token_halves(c)
                for i, p in enumerate(wide):
                    for f in range(KT):
                        at = slice(f * P, (f + 1) * P)
                        pe.wait_ge(qk_lo_done, c * 4 + i * KT + f + 1)
                        product3(pe, qk_ps[:, f, :],
                                 [(w_hi[p][:, k, at], w_lo[p][:, k, at]) for k in range(KT)],
                                 tokens).then_inc(qk_ready, 1)

        @block.scalar
        def _(act):
            norm_on_scalar(act, n)
            act.wait_ge(whole_done, len(wide))
            for i, p in enumerate(wide):
                act.activation(w_hi[p][:, :, :], whole[p][:, :, :], ACT.Copy).then_inc(w_hi_done, 1)
            act.wait_ge(bias_in, 48)
            with act.Fori(0, CHUNKS) as c:
                for i, p in enumerate(wide):
                    for f in range(KT):
                        act.wait_ge(qk_ready, c * 4 + i * KT + f + 1)
                        act.activation(attn[f"{p}_hi"][:, f, ds(c * CHUNK, CHUNK)], qk_ps[:, f, :], ACT.Identity,
                                       bias=bias[p][:, f:f + 1]).then_inc(qk_hi_done, 1)

        @block.vector
        def _(v):
            v.sem_inc(n.lo_done, FIRST)
            v.sem_inc(n.rows_out, FIRST)
            v.sem_inc(qk_lo_done, FIRST)
            for i, p in enumerate("qkv"):
                v.wait_ge(update_ready, i + 1)
                v.scalar_tensor_tensor(out=whole[p][:, :, :], in0=update_ps[:, i % 2, :, :], scalar=LORA_SCALE,
                                       in1=stage[p][:, :, :], op0=ALU.mult, op1=ALU.add).then_inc(whole_done, 1)
            v.wait_ge(bias_in, 48)

            def v_rows_out(v, j, par):
                for b in range(BATCH):
                    out = attn["v"][:, :, b, j, :, :]
                    done = v.tensor_tensor(
                        out, n.rows_ps[:, par, b * DIM:(b + 1) * DIM].rearrange("p (f h d) -> p f h d", f=KT, d=HD),
                        bias_v[:, :].rearrange("p (f h d) -> p f h d", f=KT, d=HD), ALU.add)
                done.then_inc(n.rows_out, 1)

            norm_on_vector(v, n, x_sb, v_rows_out)
            for i, p in enumerate(wide):
                v.wait_ge(w_hi_done, i + 1)
                v.tensor_tensor(w_lo[p][:, :, :], whole[p][:, :, :], w_hi[p][:, :, :].bitcast(F32),
                                ALU.subtract).then_inc(w_lo_done, 1)
            with v.Fori(0, CHUNKS) as c:
                for i, p in enumerate(wide):
                    for f in range(KT):
                        v.wait_ge(qk_hi_done, c * 4 + i * KT + f + 1)
                        at = ds(c * CHUNK, CHUNK)
                        v.scalar_tensor_tensor(out=attn[f"{p}_lo"][:, f, at], in0=qk_ps[:, f, :],
                                               scalar=bias[p][:, f:f + 1], in1=attn[f"{p}_hi"][:, f, at].bitcast(F32),
                                               op0=ALU.add, op1=ALU.subtract).then_inc(qk_lo_done, 1)


def attention_block(nc, sem, attn):
    SLOTS, HALF = 4, SEQ // 2
    ITS = KT * BATCH
    KEY_TILES = SEQ // P
    STRIP = 32
    ROWS = 4 * HD
    MAXES = 2 * KEY_TILES * 2
    STACK_DMAS = 17
    STEPS = KEY_TILES * 2
    with ExitStack() as scope:
        def sb(n, shape, dt):
            return scope.enter_context(nc.sbuf_tensor(n, shape, dt))

        def psum(n, shape, dt):
            return scope.enter_context(nc.psum_tensor(n, shape, dt))

        q_stack = [sb(f"q_stack{s}", [P, 2, SEQ], F32R) for s in range(SLOTS)]
        k_stack = [sb(f"k_stack{s}", [P, 2, SEQ], F32R) for s in range(SLOTS)]
        values = [sb(f"values{s}", [P, KEY_TILES, 2, STRIP], F32) for s in range(SLOTS)]
        probs = sb("probs", [P, 2, 2, SEQ], F32)
        maxima = sb("maxima", [P, 2, MAXES // 2, 2], F32)
        maximum = sb("maximum", [P, 2, MAXES // 2], F32)
        max_rows = sb("max_rows", [MAXES // 2, 2, P], F32R)
        mixed = sb("mixed_t", [P, HALF], F32)
        inverse = sb("inverse_sum", [P, KEY_TILES // 2, 4], F32)
        score_ps = psum("score_ps", [P, 2, SEQ], F32)
        max_ps = psum("max_ps", [P, 2, HALF], F32)
        mixed_ps = psum("mixed_ps", [P, HALF], F32)
        turn_ps = psum("turn_ps", [P, KEY_TILES // 2, 4, STRIP], F32)

        stacks_in = [sem(f"stacks_in{s}") for s in range(SLOTS)]
        max_in = [sem(f"max_in{s}") for s in range(SLOTS)]
        ones_set = sem("ones_set")
        values_in = sem("values_in")
        tile_scored = sem("tile_scored")
        tile_max = sem("tile_max")
        group_max = sem("group_max")
        max_turned = sem("max_turned")
        max_negated = sem("max_negated")
        scores_ready = sem("scores_ready")
        probs_ready = sem("probs_ready")
        probs_used = sem("probs_used")
        mixed_out = sem("mixed_out")
        mixed_turned = [sem(f"mixed_turned{s}") for s in range(SLOTS)]
        inverted = sem("inverted")
        group_out = sem("group_out")
        block = scope.enter_context(nc.Block())

        @block.sync
        def _(sp):
            sp.wait_ge(ones_set, 5 * SLOTS)
            with sp.Fori(0, ITS) as it:
                for s in range(SLOTS):
                    sp.wait_ge(mixed_turned[s], it + 1)
                    for stack, parts in ((q_stack[s], ("q_hi", "q_hi", "q_lo", "q_lo")),
                                         (k_stack[s], ("k_hi", "k_lo", "k_hi", "k_lo"))):
                        for i, part in enumerate(parts):
                            source = attn[part][:, :, :].rearrange("p f n -> p (f n)")
                            for j in range(2):
                                at = s * 2 * HD + j * HD
                                sp.dma_start(stack[i * HD:(i + 1) * HD, j, :].bitcast(F32),
                                             source[at:at + HD, ds(it * SEQ, SEQ)].bitcast(F32)).then_inc(stacks_in[s], 16)
                    sp.dma_start(q_stack[s][ROWS:ROWS + 1, :, :].bitcast(F32),
                                 q_stack[s][ROWS + 1:ROWS + 2, :, :].bitcast(F32)).then_inc(stacks_in[s], 16)

        @block.gpsimd
        def _(pool):
            for s in range(SLOTS):
                pool.memset(values[s][:, :, :, :], 0.0).then_inc(ones_set, 1)
                pool.wait_ge(ones_set, 5 * s + 1)
                pool.memset(values[s][:, :, :, HD:HD + 1], 1.0).then_inc(ones_set, 1)
                pool.wait_ge(ones_set, 5 * s + 2)
                pool.memset(q_stack[s][ROWS:P, :, :].bitcast(F32), 0.0).then_inc(ones_set, 1)
                pool.wait_ge(ones_set, 5 * s + 3)
                pool.memset(k_stack[s][ROWS:P, :, :].bitcast(F32), 0.0).then_inc(ones_set, 1)
                pool.wait_ge(ones_set, 5 * s + 4)
                pool.memset(k_stack[s][ROWS:ROWS + 1, :, :].bitcast(F32), 1.0).then_inc(ones_set, 1)
                pool.wait_ge(ones_set, 5 * s + 5)
            by_group = attn["v"][:, :, :, :, :, :].rearrange("p f b j h d -> p (f b) j (h d)")
            with pool.Fori(0, ITS) as it:
                for s in range(SLOTS):
                    pool.wait_ge(mixed_turned[s], it + 1)
                    pool.tensor_copy(values[s][:, :, :, 0:HD],
                                     by_group[:, it, :, s * 2 * HD:(s + 1) * 2 * HD]
                                     .rearrange("p j (h d) -> p j h d", d=HD)).then_inc(values_in, 1)

        @block.tensor
        def _(pe):
            ident = attn["ident"]

            def max_scores(group, s, indices):
                for i in indices:
                    j, qt, half = i // 16, i // 2 % KEY_TILES, i % 2
                    if isinstance(group, int) and group * MAXES + i < 2:
                        pass
                    else:
                        pe.wait_ge(tile_max, group * MAXES + i - 1)
                    pe.matmul(max_ps[:, i % 2, :], q_stack[s][:, j, qt * P:(qt + 1) * P],
                              k_stack[s][:, j, half * HALF:(half + 1) * HALF], start=True, stop=True
                              ).then_inc(tile_scored, 1)

            def turn_group_max(count, par, groups_out):
                pe.wait_ge(group_max, count)
                pe.wait_ge(group_out, groups_out + 1)
                pe.transpose(turn_ps[0:MAXES // 2, :, :, :].rearrange("p a b c -> p (a b c)")[:, 0:P],
                             maximum[:, par, :], ident).then_inc(max_turned, 1)

            def slot(it, s, last):
                group = it * SLOTS + s
                ahead_slot, ahead_it = (s + 2) % SLOTS, it + (s + 2) // SLOTS
                has_ahead = not (last and s + 2 >= SLOTS)
                has_next = not (last and s + 1 >= SLOTS)

                def ahead(step):
                    if has_ahead:
                        max_scores(group + 2, ahead_slot, range(4 * step, 4 * step + 4))

                def score(kt):
                    for j in range(2):
                        n = kt * 2 + j
                        if n >= 2:
                            pe.wait_ge(probs_ready, group * STEPS + n - 1)
                        for half in range(2):
                            at = slice(half * HALF, (half + 1) * HALF)
                            mm = pe.matmul(score_ps[:, j, at], k_stack[s][:, j, kt * P:(kt + 1) * P],
                                           q_stack[s][:, j, at], start=True, stop=True)
                        mm.then_inc(scores_ready, 1)

                def mix(kt):
                    pe.wait_ge(probs_ready, group * STEPS + kt * 2 + 2)
                    if kt == 0:
                        pe.wait_ge(mixed_out, group + 1)
                        pe.wait_ge(values_in, group + 1)
                    for j in range(2):
                        for half in range(2):
                            strip = (j * 2 + half) * STRIP
                            mm = pe.matmul(mixed_ps[strip:strip + STRIP, :], values[s][:, kt, j, :],
                                           probs[:, kt % 2, j, half * HALF:(half + 1) * HALF],
                                           start=(kt == 0), stop=(kt == KEY_TILES - 1),
                                           tile_position=(0, strip))
                    mm.then_inc(probs_used, 1)

                pe.wait_ge(max_in[s], (it + 1) * 16)
                if has_ahead:
                    pe.wait_ge(stacks_in[ahead_slot], (ahead_it + 1) * STACK_DMAS * 16)
                score(0)
                ahead(0)
                for kt in range(1, KEY_TILES):
                    score(kt)
                    if kt == 1 and has_next:
                        turn_group_max(group + 2, (s + 1) % 2, group * 2)
                    if kt < KEY_TILES - 1:
                        ahead(kt)
                    mix(kt - 1)
                mix(KEY_TILES - 1)
                ahead(KEY_TILES - 1)
                pe.wait_ge(mixed_out, group + 2)
                if has_next:
                    pe.wait_ge(max_negated, group + 2)
                else:
                    pe.wait_ge(group_out, group * 2 + 1)
                for qt in range(KEY_TILES // 2):
                    turn = pe.transpose(turn_ps[:, qt, :, :].rearrange("p a b -> p (a b)"),
                                        mixed[:, qt * P:(qt + 1) * P], ident)
                turn.then_inc(mixed_turned[s], 1)

            for s in range(SLOTS):
                pe.sem_inc(mixed_turned[s], 1)
            pe.wait_ge(ones_set, 5 * SLOTS)
            pe.wait_ge(stacks_in[0], STACK_DMAS * 16)
            max_scores(0, 0, range(MAXES))
            pe.wait_ge(stacks_in[1], STACK_DMAS * 16)
            max_scores(1, 1, range(4))
            turn_group_max(1, 0, 0)
            max_scores(1, 1, range(4, MAXES))
            with pe.Fori(0, ITS - 1) as it:
                for s in range(SLOTS):
                    slot(it, s, False)
            for s in range(SLOTS):
                slot(ITS - 1, s, True)

        @block.scalar
        def _(act):
            def negate_maxima(count, par, s, max_it):
                act.wait_ge(max_turned, count)
                act.activation(max_rows[:, par, :],
                               turn_ps[0:MAXES // 2, :, :, :].rearrange("p a b c -> p (a b c)")[:, 0:P],
                               ACT.Copy, scale=-1.0).then_inc(max_negated, 1)
                act.wait_ge(max_negated, count)
                act.dma_start(q_stack[s][ROWS:ROWS + 1, :, :].rearrange("o j (t q) -> o (j t) q", q=P).bitcast(F32),
                              max_rows[:, par, :].bitcast(F32)).then_inc(max_in[s], 16)

            def slot(it, s, last):
                group = it * SLOTS + s
                has_next = not (last and s + 1 >= SLOTS)
                for n in range(STEPS):
                    act.wait_ge(scores_ready, group * STEPS + n + 1)
                    if n >= 4:
                        act.wait_ge(probs_used, group * KEY_TILES + n // 2 - 1)
                    act.activation(probs[:, n // 2 % 2, n % 2, :], score_ps[:, n % 2, :], ACT.Exp, scale=SCORE_SCALE
                                   ).then_inc(probs_ready, 1)
                    if n == 3 and has_next:
                        negate_maxima(group + 2, (s + 1) % 2, (s + 1) % SLOTS, it)
                act.wait_ge(probs_used, (group + 1) * KEY_TILES)
                act.activation(mixed[:, :], mixed_ps[:, :], ACT.Copy).then_inc(mixed_out, 1)

            act.sem_inc(mixed_out, 1)
            negate_maxima(1, 0, 0, 0)
            with act.Fori(0, ITS - 1) as it:
                for s in range(SLOTS):
                    slot(it, s, False)
            for s in range(SLOTS):
                slot(ITS - 1, s, True)

        @block.vector
        def _(v):
            def take_maxima(group, par, indices):
                for i in indices:
                    v.wait_ge(tile_scored, group * MAXES + i + 1)
                    v.reduce_max(maxima[:, par, i // 2, i % 2:i % 2 + 1], max_ps[:, i % 2, :], axis=AXIS_X
                                 ).then_inc(tile_max, 1)

            def close_maxima(group, par):
                v.wait_ge(tile_max, (group + 1) * MAXES)
                v.tensor_tensor(maximum[:, par, :], maxima[:, par, :, 0], maxima[:, par, :, 1], ALU.max
                                ).then_inc(group_max, 1)

            def write_out(it, s):
                group = it * SLOTS + s
                v.wait_ge(mixed_turned[s], it + 2)
                v.reciprocal(inverse[:, :, :], turn_ps[:, :, :, HD]).then_inc(inverted, 1)
                v.wait_ge(inverted, group + 1)
                for j in range(2):
                    at = s * 2 * HD + j * HD
                    v.tensor_tensor(
                        attn["out"][:, it, :, at:at + HD].rearrange("p (half t) d -> p half t d", half=2),
                        turn_ps[:, :, 2 * j:2 * j + 2, 0:HD].rearrange("p t half d -> p half t d"),
                        inverse[:, :, 2 * j:2 * j + 2].rearrange("p t half -> p half t").unsqueeze(3)
                        .broadcast_to([P, 2, KEY_TILES // 2, HD]),
                        ALU.mult).then_inc(group_out, 1)

            def slot(it, s, last):
                group = it * SLOTS + s
                if not (last and s + 2 >= SLOTS):
                    take_maxima(group + 2, s % 2, range(MAXES))
                    close_maxima(group + 2, s % 2)
                write_out(it, s)

            v.sem_inc(group_out, 1)
            for group in range(2):
                take_maxima(group, group, range(MAXES))
                close_maxima(group, group)
            with v.Fori(0, ITS - 1) as it:
                for s in range(SLOTS):
                    slot(it, s, False)
            for s in range(SLOTS):
                slot(ITS - 1, s, True)


def output_block(nc, sem, dram, keep, attn):
    x_sb, ident = keep["x"], keep["ident"]
    with ExitStack() as scope:
        def sb(n, shape, dt):
            return scope.enter_context(nc.sbuf_tensor(f"o_{n}", shape, dt))

        def psum(n, shape, dt):
            return scope.enter_context(nc.psum_tensor(f"o_{n}", shape, dt))

        stage = sb("stage", [P, KT, DIM], F32)
        w_o = sb("w", [P, KT, DIM], F32)
        bias_o = sb("bias", [P, DIM], F32)
        lora_b, lora_a = sb("lora_b", [RANK, DIM], F32), sb("lora_a", [RANK, DIM], F32)
        rows = sb("rows", [P, 2, DIM], F32)
        columns = sb("columns", [P, 2, KT, P], F32)
        biased = sb("biased", [P, 2, DIM], F32)
        update_ps = psum("update_ps", [P, 2, DIM], F32)
        columns_ps = psum("columns_ps", [P, 2, 512], F32)
        out_ps = psum("out_ps", [P, 2, 512], F32)

        weights_in, bias_in = sem("o_weights_in"), sem("o_bias_in")
        update_ready, whole_done = sem("o_update_ready"), sem("o_whole_done")
        rows_done = sem("o_rows_done")
        turned = sem("o_turned")
        columns_done = sem("o_columns_done")
        out_ready = sem("o_out_ready")
        biased_done = sem("o_biased_done")
        x_updated = sem("o_x_updated")
        block = scope.enter_context(nc.Block())

        @block.sync
        def _(sp):
            sp.dma_start(stage[:, :, :], dram["wo_t"].rearrange("(k p) o -> p k o", p=P)).then_inc(weights_in, 16)
            sp.dma_start(lora_b[:, :], dram["lora_bo"]).then_inc(weights_in, 16)
            sp.dma_start(lora_a[:, :], dram["lora_ao_t"]).then_inc(weights_in, 16)
            sp.dma_start(bias_o[:, :], dram["bo"].partition_broadcast(P)).then_inc(bias_in, 16)

        @block.tensor
        def _(pe):
            pe.sem_inc(turned, FIRST)
            pe.sem_inc(out_ready, FIRST)
            pe.wait_ge(weights_in, 48)
            for k in range(KT):
                update = pe.matmul(update_ps[:, k, :], lora_b[:, k * P:(k + 1) * P], lora_a[:, :],
                                   start=True, stop=True)
            update.then_inc(update_ready, 1)
            pe.wait_ge(whole_done, 1)
            with pe.Fori(0, TILES // 2) as pair:
                for par in range(2):
                    t = pair * 2 + par
                    pe.wait_ge(rows_done, t + 1)
                    pe.wait_ge(columns_done, t + 1)
                    for k in range(KT):
                        turn = pe.transpose(columns_ps[:, par, k * P:(k + 1) * P], rows[:, par, k * P:(k + 1) * P],
                                            ident[:, :])
                    turn.then_inc(turned, 1)
                for par in range(2):
                    t = pair * 2 + par
                    pe.wait_ge(columns_done, t + 1 + FIRST)
                    pe.wait_ge(x_updated, t + 1)
                    for k in range(KT):
                        out = pe.matmul(out_ps[:, par, 0:DIM], columns[:, par, k, :], w_o[:, k, :],
                                        start=(k == 0), stop=(k == KT - 1))
                    out.then_inc(out_ready, 1)

        @block.scalar
        def _(act):
            act.sem_inc(columns_done, FIRST)
            by_tile = attn["out"][:, :, :, :].rearrange("p (f b) j d -> p f (b j) d", f=KT)
            with act.Fori(0, TILES // 2) as pair:
                for par in range(2):
                    t = pair * 2 + par
                    act.wait_ge(turned, t + 1)
                    act.activation(rows[:, par, :].rearrange("p (f d) -> p f d", f=KT), by_tile[:, :, t, :],
                                   ACT.Copy).then_inc(rows_done, 1)
                for par in range(2):
                    t = pair * 2 + par
                    act.wait_ge(turned, t + 1 + FIRST)
                    act.wait_ge(out_ready, t + 1)
                    act.activation(columns[:, par, :, :].rearrange("p k q -> p (k q)"), columns_ps[:, par, 0:DIM],
                                   ACT.Copy).then_inc(columns_done, 1)

        @block.vector
        def _(v):
            v.sem_inc(x_updated, FIRST)
            v.wait_ge(update_ready, 1)
            v.scalar_tensor_tensor(out=w_o[:, :, :], in0=update_ps[:, :, :], scalar=LORA_SCALE,
                                   in1=stage[:, :, :], op0=ALU.mult, op1=ALU.add).then_inc(whole_done, 1)
            v.wait_ge(bias_in, 16)
            with v.Fori(0, TILES // 2) as pair:
                for par in range(2):
                    t = pair * 2 + par
                    v.wait_ge(x_updated, t + 1)
                    v.tensor_tensor(biased[:, par, :], x_sb[:, t, :], bias_o[:, :], ALU.add).then_inc(biased_done, 1)
                for par in range(2):
                    t = pair * 2 + par
                    v.wait_ge(biased_done, t + 1)
                    v.wait_ge(out_ready, t + 1 + FIRST)
                    v.tensor_tensor(x_sb[:, t, :], out_ps[:, par, 0:DIM], biased[:, par, :], ALU.add
                                    ).then_inc(x_updated, 1)


def attention(nc, sem, dram, keep):
    with ExitStack() as scope:
        def sb(name, shape, dt):
            return scope.enter_context(nc.sbuf_tensor(name, shape, dt))

        attn = {"ident": keep["ident"][:, :], "out": sb("attn_out", [P, KT * BATCH, JT, P], F32)}
        with ExitStack() as inner:
            for part in ("q_hi", "q_lo", "k_hi", "k_lo"):
                attn[part] = inner.enter_context(nc.sbuf_tensor(part, [P, KT, TOKENS], F32R))
            attn["v"] = inner.enter_context(nc.sbuf_tensor("v_rows", [P, KT, BATCH, JT, HEADS // KT, HD], F32))
            project_block(nc, sem, dram, keep, attn)
            attention_block(nc, sem, attn)
        output_block(nc, sem, dram, keep, attn)


def macaron(nc, dram):
    with ExitStack() as outer:
        def sb(name, shape, dt):
            return outer.enter_context(nc.sbuf_tensor(name, shape, dt))

        def sem(name):
            return outer.enter_context(nc.semaphore(name))

        keep = {
            "x": sb("x_sb", [P, TILES, DIM], F32),
            "ident": sb("ident", [P, P], F32),
            "minus_half": sb("minus_half", [P, TILES], F32),
            "route_w": sb("route_w", [P, KT, 2, 2, KEYS], F32),
            "x_in": sem("x_in"),
            "ident_done": sem("ident_done"),
        }
        setup_block(nc, outer, sem, dram, keep)
        ffn_block(nc, sem, dram, keep, 0)
        attention(nc, sem, dram, keep)
        ffn_block(nc, sem, dram, keep, 1)


def kernel(L0_attn_x, L0_attn_Wq, L0_attn_bq, L0_attn_Bq, L0_attn_Aq, L0_attn_Wk, L0_attn_bk, L0_attn_Bk,
           L0_attn_Ak, L0_attn_Wv, L0_attn_bv, L0_attn_Bv, L0_attn_Av, L0_attn_Wo, L0_attn_bo, L0_attn_Bo,
           L0_attn_Ao, L0_ffn_W_q, L0_ffn_keys, L0_ffn_down_embed, L0_ffn_up_embed, L0_ffn_gate_w,
           L0_ffn_up_w, L0_ffn_down_w):
    import numpy as np
    import concourse.bacc as bacc
    from concourse.bass_utils import run_bass_kernel_spmd

    nc = bacc.Bacc("TRN2", target_bir_lowering=False, num_devices=1)
    laid = {
        "x": np.asarray(L0_attn_x).reshape(TOKENS, DIM),
        "retrieval_t": np.asarray(L0_ffn_W_q).T, "keys": L0_ffn_keys,
        "gate": L0_ffn_gate_w, "up": L0_ffn_up_w, "down": L0_ffn_down_w,
        "down_embed": np.asarray(L0_ffn_down_embed).T, "up_embed": L0_ffn_up_embed,
    }
    for p, (w, b, bm, am) in {"q": (L0_attn_Wq, L0_attn_bq, L0_attn_Bq, L0_attn_Aq),
                              "k": (L0_attn_Wk, L0_attn_bk, L0_attn_Bk, L0_attn_Ak),
                              "v": (L0_attn_Wv, L0_attn_bv, L0_attn_Bv, L0_attn_Av),
                              "o": (L0_attn_Wo, L0_attn_bo, L0_attn_Bo, L0_attn_Ao)}.items():
        laid |= {f"w{p}_t": np.asarray(w).T, f"b{p}": b, f"lora_b{p}": bm, f"lora_a{p}_t": np.asarray(am).T}
        if p in "qk":
            laid[f"b{p}_columns"] = np.asarray(b).reshape(KT, P).T
    arrays, dram = {}, {}
    for name, a in laid.items():
        arrays[f"in_{name}"] = a = np.ascontiguousarray(a)
        dram[name] = nc.dram_tensor(f"in_{name}", a.shape, mybir.dt.from_np(a.dtype), kind="ExternalInput").ap()
    dram["out"] = nc.dram_tensor("out", (TOKENS, DIM), F32, kind="ExternalOutput").ap()
    macaron(nc, dram)
    r = run_bass_kernel_spmd(nc, [arrays], core_ids=[0])
    return np.asarray(r.results[0]["out"]).reshape(BATCH, SEQ, DIM)
```

```python
from contextlib import ExitStack

import concourse.bass as bass
from concourse import mybir

F32 = mybir.dt.float32
F32R = mybir.dt.float32r
ALU = mybir.AluOpType
ACT = mybir.ActivationFunctionType
AXIS_X = mybir.AxisListType.X
ds = bass.ds

P = 128
BATCH, SEQ, DIM = 2, 1024, 256
TOKENS = BATCH * SEQ
KT = DIM // P
TILES = TOKENS // P
JT = SEQ // P
CHUNK = 512
CHUNKS = TOKENS // CHUNK
CT = CHUNK // P
HEADS, HD, RANK = 16, 16, 16
LORA_SCALE = 8.0 / RANK
SCORE_SCALE = HD ** -0.5
INTER, EXPERTS, KEYS, RETRIEVAL, TOP = 1024, 512, 64, 128, 8
GRID_ROWS = EXPERTS // KEYS
FT = INTER // P
ET = EXPERTS // P
UNITS = FT + ET
EPS = 1e-5
FIRST = 2


def product3(pe, out, w, x):
    last = len(w) - 1
    for k, ((w_hi, w_lo), (x_hi, x_lo)) in enumerate(zip(w, x)):
        pe.matmul(out, w_hi, x_hi, start=(k == 0), stop=False)
        pe.matmul(out, w_lo, x_hi, start=False, stop=False)
        done = pe.matmul(out, w_hi, x_lo, start=False, stop=(k == last))
    return done


class Norm:

    def __init__(self, name, sb, psum, sem, halves, rows_width):
        self.xhi, self.xlo = halves
        self.work = sb(f"{name}_work", [P, 4, TILES], F32)
        self.mean = sb(f"{name}_mean", [P, TILES], F32)
        self.var = sb(f"{name}_var", [P, TILES], F32)
        self.rstd = sb(f"{name}_rstd", [P, TILES], F32)
        self.xn = sb(f"{name}_xn", [P, 2, BATCH, DIM], F32)
        self.full = sb(f"{name}_full", [P, 2, KT, BATCH, P], F32)
        self.turned_ps = psum(f"{name}_turned", [P, 2, KT, BATCH, P], F32)
        self.rows_ps = psum(f"{name}_rows", [P, 2, 512], F32)
        self.rows_width = rows_width
        self.var_done = sem(f"{name}_var_done")
        self.rstd_done = sem(f"{name}_rstd_done")
        self.xn_done = sem(f"{name}_xn_done")
        self.turned = sem(f"{name}_turned_done")
        self.full_done = sem(f"{name}_full_done")
        self.hi_done = sem(f"{name}_hi_done")
        self.lo_done = sem(f"{name}_lo_done")
        self.rows_done = sem(f"{name}_rows_done")
        self.rows_out = sem(f"{name}_rows_out")

    def token_halves(self, c):
        hi = self.xhi[:, :, :, :].rearrange("p k b s -> p k (b s)")
        lo = self.xlo[:, :, :, :].rearrange("p k b s -> p k (b s)")
        return [(hi[:, k, ds(c * CHUNK, CHUNK)], lo[:, k, ds(c * CHUNK, CHUNK)]) for k in range(KT)]


def norm_on_vector(v, n, x_sb, stats, rows_evacuation=None):
    even_mean, odd_mean = stats[:, :, 1], stats[:, :, 4]
    even_m2, odd_m2 = stats[:, :, 2], stats[:, :, 5]
    v.tensor_tensor(n.work[:, 0, :], even_mean, odd_mean, ALU.add).then_inc(n.var_done, 1)
    v.tensor_tensor(n.work[:, 1, :], even_mean, odd_mean, ALU.subtract).then_inc(n.var_done, 1)
    v.tensor_tensor(n.work[:, 2, :], even_m2, odd_m2, ALU.add).then_inc(n.var_done, 1)
    v.wait_ge(n.var_done, 3)
    v.tensor_scalar(n.mean[:, :], n.work[:, 0, :], 0.5, None, ALU.mult).then_inc(n.var_done, 1)
    v.tensor_tensor(n.work[:, 3, :], n.work[:, 1, :], n.work[:, 1, :], ALU.mult).then_inc(n.var_done, 1)
    v.wait_ge(n.var_done, 5)
    v.tensor_scalar(n.work[:, 0, :], n.work[:, 3, :], 0.25, EPS, ALU.mult, ALU.add).then_inc(n.var_done, 1)
    v.wait_ge(n.var_done, 6)
    v.scalar_tensor_tensor(out=n.var[:, :], in0=n.work[:, 2, :], scalar=1.0 / DIM, in1=n.work[:, 0, :],
                           op0=ALU.mult, op1=ALU.add).then_inc(n.var_done, 1)
    v.wait_ge(n.rstd_done, 1)

    def normalize(j, par):
        v.wait_ge(n.turned, j + 1)
        for b in range(BATCH):
            t = b * JT + j
            v.tensor_scalar(n.xn[:, par, b, :], x_sb[:, t, :], n.mean[:, ds(t, 1)], n.rstd[:, ds(t, 1)],
                            ALU.subtract, ALU.mult).then_inc(n.xn_done, 1)

    def low_parts(j, par):
        at = ds(j * P, P)
        v.wait_ge(n.hi_done, j + 1)
        v.tensor_tensor(n.xlo[:, :, :, at], n.turned_ps[:, par, :, :, :], n.xhi[:, :, :, at].bitcast(F32),
                        ALU.subtract).then_inc(n.lo_done, 1)

    def rows_out(j, par):
        if rows_evacuation is not None:
            v.wait_ge(n.rows_done, j + 1 + FIRST)
            rows_evacuation(v, j, par)

    normalize(0, 0)
    normalize(1, 1)
    with v.Fori(0, JT // 2 - 1) as pair:
        for par in range(2):
            j = pair * 2 + par
            low_parts(j, par)
            normalize(j + 2, par)
            rows_out(j, par)
    for par in range(2):
        low_parts(JT - 2 + par, par)
        rows_out(JT - 2 + par, par)


def norm_on_gpsimd(pool, n, minus_half):
    pool.wait_ge(n.var_done, 7)
    pool.tensor_tensor(n.rstd[:, :], n.var[:, :], minus_half, ALU.pow).then_inc(n.rstd_done, 1)


def norm_on_tensor(pe, n, ident, rows_weights):
    pe.sem_inc(n.turned, FIRST)
    pe.sem_inc(n.rows_done, FIRST)

    def turn(j, par):
        pe.wait_ge(n.xn_done, (j + 1) * BATCH)
        pe.wait_ge(n.lo_done, j + 1)
        for k in range(KT):
            for b in range(BATCH):
                turned = pe.transpose(n.turned_ps[:, par, k, b, :], n.xn[:, par, b, k * P:(k + 1) * P], ident)
        turned.then_inc(n.turned, 1)

    def rows_product(j, par):
        pe.wait_ge(n.full_done, j + 1)
        pe.wait_ge(n.rows_out, j + 1)
        w = n.rows_width
        for b in range(BATCH):
            for k in range(KT):
                rows = pe.matmul(n.rows_ps[:, par, b * w:(b + 1) * w], n.full[:, par, k, b, :],
                                 rows_weights(k, b), start=(k == 0), stop=(k == KT - 1))
        rows.then_inc(n.rows_done, 1)

    turn(0, 0)
    with pe.Fori(0, JT // 2 - 1) as pair:
        for par in range(2):
            j = pair * 2 + par
            turn(j + 1, 1 - par)
            rows_product(j, par)
    turn(JT - 1, 1)
    rows_product(JT - 2, 0)
    rows_product(JT - 1, 1)


def norm_on_scalar(act, n, rows_evacuation=None):
    def copies(j, par):
        act.wait_ge(n.turned, j + 1 + FIRST)
        act.wait_ge(n.rows_done, j + 1)
        act.activation(n.full[:, par, :, :, :], n.turned_ps[:, par, :, :, :], ACT.Copy).then_inc(n.full_done, 1)
        act.activation(n.xhi[:, :, :, ds(j * P, P)], n.turned_ps[:, par, :, :, :], ACT.Copy).then_inc(n.hi_done, 1)

    def rows_out(j, par):
        if rows_evacuation is not None:
            act.wait_ge(n.rows_done, j + 1 + FIRST)
            rows_evacuation(act, j, par)

    copies(0, 0)
    with act.Fori(0, JT // 2 - 1) as pair:
        for par in range(2):
            j = pair * 2 + par
            copies(j + 1, 1 - par)
            rows_out(j, par)
    copies(JT - 1, 1)
    rows_out(JT - 2, 0)
    rows_out(JT - 1, 1)


def setup_block(nc, outer, sem, dram, keep):
    with ExitStack() as scope:
        def sb(name, shape, dt):
            return scope.enter_context(nc.sbuf_tensor(name, shape, dt))

        wq_rows = sb("wq_rows", [RETRIEVAL // 2, 2, DIM], F32)
        keys_sb = sb("keys_sb", [RETRIEVAL // 2, 2, KEYS], F32)
        fold_ps = scope.enter_context(nc.psum_tensor("fold_ps", [P, KT, 2, 2, KEYS], F32))
        wq_in, keys_in = sem("wq_in"), sem("keys_in")
        x_in = [sem(f"x_in{c}") for c in range(CHUNKS)]
        ident_zero, folded, fold_out = sem("ident_zero"), sem("folded"), sem("fold_out")
        block = scope.enter_context(nc.Block())

        @block.sync
        def _(sp):
            sp.dma_start(wq_rows[:, :, :], dram["retrieval_t"].rearrange("(h d) x -> d h x", h=2)).then_inc(wq_in, 16)
            sp.dma_start(keys_sb[:, :, :], dram["keys"].rearrange("t d k -> d t k")).then_inc(keys_in, 16)
            x_tiles = dram["x"].rearrange("(t p) d -> p t d", p=P)
            for c in range(CHUNKS):
                sp.dma_start(keep["x"][:, c * CT:(c + 1) * CT, :], x_tiles[:, c * CT:(c + 1) * CT, :]
                             ).then_inc(x_in[c], 16)

        @block.gpsimd
        def _(pool):
            pool.memset(keep["ident"][:, :], 0.0).then_inc(ident_zero, 1)
            pool.memset(keep["minus_half"][:, :], -0.5).then_inc(keep["ident_done"], 1)
            pool.wait_ge(ident_zero, 1)
            pool.affine_select(out=keep["ident"][:, :], in_=keep["ident"][:, :], compare_op=ALU.not_equal,
                               fill=1.0, base=0, pattern=[[-1, P]], channel_multiplier=1
                               ).then_inc(keep["ident_done"], 1)

        @block.tensor
        def _(pe):
            pe.wait_ge(wq_in, 16)
            pe.wait_ge(keys_in, 16)
            for half in range(2):
                for k in range(KT):
                    for t in range(2):
                        fold = pe.matmul(fold_ps[:, k, t, half, :], wq_rows[:, half, k * P:(k + 1) * P],
                                         keys_sb[:, t, :], start=True, stop=True)
            fold.then_inc(folded, 1)

        @block.vector
        def _(v):
            v.wait_ge(folded, 1)
            v.tensor_copy(keep["route_w"][:, :, :, :, :], fold_ps[:, :, :, :, :]).then_inc(fold_out, 1)
            for c in range(CHUNKS):
                v.wait_ge(x_in[c], 16)
                for t in range(c * CT, (c + 1) * CT):
                    v.bn_stats(keep["stats"][:, t, :], keep["x"][:, t, :]).then_inc(keep["stats_done"], 1)


def ffn_block(nc, sem_of, dram, keep, layer):
    store = layer == 1
    x_sb, ident = keep["x"], keep["ident"]
    name = f"ffn{layer}"
    with ExitStack() as scope:
        def sb(n, shape, dt):
            return scope.enter_context(nc.sbuf_tensor(f"{name}_{n}", shape, dt))

        def psum(n, shape, dt):
            return scope.enter_context(nc.psum_tensor(f"{name}_{n}", shape, dt))

        def sem(n):
            return sem_of(f"{name}_{n}")

        parts = (("gate", INTER), ("up", INTER), ("down_embed", EXPERTS))
        hi = {w: sb(f"{w}_hi", [P, KT, n], F32R) for w, n in parts}
        lo = {w: sb(f"{w}_lo", [P, KT, n], F32R) for w, n in parts}
        down = sb("down", [P, FT, DIM], F32)
        up_embed = sb("up_embed", [P, ET, DIM], F32)
        routes = sb("routes", [P, JT, 2, 2, KEYS], F32)
        hidden = sb("hidden", [P, UNITS, CHUNK], F32)
        tanh = sb("tanh", [P, 2, CHUNK], F32)
        gated = sb("gated", [P, 2, CHUNK], F32)
        mix = sb("mix", [P, 2, 2, EXPERTS], F32)
        r = sb("r", [P, 2, 2, 2, KEYS], F32)
        best = sb("best", [P, 2, 2, 2, TOP], F32)
        below = sb("below", [P, 2, 2, 2, KEYS], F32)
        expo = sb("expo", [P, 2, 2, 2, KEYS], F32)
        pairs = sb("pairs", [P, 2, 2, TOP, TOP], F32)
        top = sb("top", [P, 2, 2, TOP], F32)
        top_below = sb("top_below", [P, 2, 2, TOP], F32)
        top_exp = sb("top_exp", [P, 2, 2, TOP], F32)
        total = sb("total", [P, 2, 2], F32)
        inverse = sb("inverse", [P, 2, 2], F32)
        row_exp = sb("row_exp", [P, 2, 2, GRID_ROWS], F32)
        sums = sb("sums", [P, 2, 2, GRID_ROWS, KEYS], F32)
        grid = sb("grid", [P, 2, 2, GRID_ROWS, KEYS], F32)
        inside = sb("inside", [P, 2, 2], F32)
        clipped = sb("clipped", [P, 2, 2], F32)

        halves = [sb(f"x{part}", [P, KT, BATCH, SEQ], F32R) for part in ("hi", "lo")]

        part_in = {w: sem(f"{w}_in") for w, _ in parts}
        down_in, up_embed_in = sem("down_in"), sem("up_embed_in")
        part_hi, part_lo = sem("part_hi"), sem("part_lo")
        route_in = sem("route_in")
        scored = sem("scored")
        route_exp = sem("route_exp")
        scaled = sem("scaled")
        grid_done = sem("grid_done")
        mixed = sem("mixed")
        gate_ready, up_ready = sem("gate_ready"), sem("up_ready")
        tanh_done, gated_done, hidden_done = sem("tanh_done"), sem("gated_done"), sem("hidden_done")
        mix_turned, out_ready, x_updated = sem("mix_turned"), sem("out_ready"), sem("x_updated")
        stored = sem("stored")

        with ExitStack() as norm_scope:
            def norm_sb(n, shape, dt):
                return norm_scope.enter_context(nc.sbuf_tensor(n, shape, dt))

            def norm_psum(n, shape, dt):
                return norm_scope.enter_context(nc.psum_tensor(n, shape, dt))

            stage = {w: norm_scope.enter_context(nc.sbuf_tensor(f"{name}_{w}_stage", [P, KT, n], F32))
                     for w, n in parts}
            n = Norm(f"{name}_norm", norm_sb, norm_psum, sem_of, halves, KEYS * 2)
            block = norm_scope.enter_context(nc.Block())

            @block.sync
            def _(sp):
                for w, _ in parts:
                    sp.dma_start(stage[w][:, :, :], dram[w].rearrange("(k p) f -> p k f", p=P)
                                 ).then_inc(part_in[w], 16)
                sp.dma_start(down[:, :, :], dram["down"].rearrange("(f p) d -> p f d", p=P)).then_inc(down_in, 16)
                sp.dma_start(up_embed[:, :, :], dram["up_embed"].rearrange("(f p) d -> p f d", p=P)
                             ).then_inc(up_embed_in, 16)

            @block.gpsimd
            def _(pool):
                norm_on_gpsimd(pool, n, keep["minus_half"][:, :])
                for i, (w, _) in enumerate(parts):
                    pool.wait_ge(part_hi, i + 1)
                    pool.tensor_tensor(lo[w][:, :, :], stage[w][:, :, :], hi[w][:, :, :].bitcast(F32),
                                       ALU.subtract).then_inc(part_lo, 1)

            @block.tensor
            def _(pe):
                pe.wait_ge(keep["ident_done"], 2)
                norm_on_tensor(pe, n, ident[:, :],
                               lambda k, b: keep["route_w"][:, k, b, :, :].rearrange("p h k -> p (h k)"))

            @block.scalar
            def _(act):
                act.sem_inc(n.rows_out, FIRST)

                def routes_out(act, j, par):
                    act.activation(routes[:, j, :, :, :],
                                   n.rows_ps[:, par, 0:4 * KEYS].rearrange("p (b h k) -> p b h k", b=2, h=2),
                                   ACT.Copy).then_inc(n.rows_out, 1)

                for w, _ in parts:
                    act.wait_ge(part_in[w], 16)
                    act.activation(hi[w][:, :, :], stage[w][:, :, :], ACT.Copy).then_inc(part_hi, 1)
                norm_on_scalar(act, n, routes_out)

            @block.vector
            def _(v):
                v.sem_inc(n.lo_done, FIRST)
                norm_on_vector(v, n, x_sb, keep["stats"])

        gate_ps = psum("gate_ps", [P, 2, CHUNK], F32)
        up_ps = psum("up_ps", [P, 2, CHUNK], F32)
        mix_ps = psum("mix_ps", [P, 2, CHUNK], F32)
        out_ps = psum("out_ps", [P, 2, 512], F32)
        block = scope.enter_context(nc.Block())
        SCORE_STEPS, SCALE_STEPS, MIX_STEPS = 11, 3, 4
        EXPS_AFTER = (2, 4)

        def weight(w, i):
            at = slice(i * P, (i + 1) * P)
            return [(hi[w][:, k, at], lo[w][:, k, at]) for k in range(KT)]

        @block.tensor
        def _(pe):
            pe.wait_ge(part_lo, len(parts))
            with pe.Fori(0, CHUNKS) as c:
                tokens = n.token_halves(c)
                for u in range(FT):
                    if u >= 2:
                        pe.wait_ge(hidden_done, c * UNITS + u - 1)
                    product3(pe, gate_ps[:, u % 2, :], weight("gate", u), tokens).then_inc(gate_ready, 1)
                    product3(pe, up_ps[:, u % 2, :], weight("up", u), tokens).then_inc(up_ready, 1)
                def expert_product(e):
                    pe.wait_ge(gated_done, c * UNITS + FT + e - 1)
                    product3(pe, gate_ps[:, e % 2, :], weight("down_embed", e), tokens).then_inc(gate_ready, 1)

                def turn_mix(e):
                    if e >= 2:
                        pe.wait_ge(hidden_done, c * UNITS + FT + e - 1)
                    for jh in range(4):
                        turn = pe.transpose(mix_ps[:, e % 2, jh * P:(jh + 1) * P],
                                            mix[:, jh // 2, jh % 2, e * P:(e + 1) * P], ident[:, :])
                    turn.then_inc(mix_turned, 1)

                expert_product(0)
                expert_product(1)
                pe.wait_ge(mixed, (c + 1) * 2 * MIX_STEPS)
                turn_mix(0)
                turn_mix(1)
                for e in range(2, ET):
                    expert_product(e)
                    turn_mix(e)
                pe.wait_ge(down_in, 16)
                pe.wait_ge(up_embed_in, 16)
                for tt in range(CT):
                    if tt >= 2:
                        pe.wait_ge(x_updated, c * CT + tt - 1)
                    for u in range(UNITS):
                        if tt == 0:
                            pe.wait_ge(hidden_done, c * UNITS + u + 1)
                        rhs = down[:, u, :] if u < FT else up_embed[:, u - FT, :]
                        out = pe.matmul(out_ps[:, tt % 2, 0:DIM], hidden[:, u, tt * P:(tt + 1) * P], rhs,
                                        start=(u == 0), stop=(u == UNITS - 1))
                    out.then_inc(out_ready, 1)

        @block.scalar
        def _(act):
            def fetch_routes(j, jp):
                act.activation(r[:, jp, :, :, :], routes[:, j, :, :, :], ACT.Copy).then_inc(route_in, 1)

            def route_exps(j, jp):
                act.wait_ge(scored, (j + 1) * SCORE_STEPS)
                act.activation(expo[:, jp, :, :, :], below[:, jp, :, :, :], ACT.Exp).then_inc(route_exp, 1)
                act.activation(top_exp[:, jp, :, :], top_below[:, jp, :, :], ACT.Exp).then_inc(route_exp, 1)

            with act.Fori(0, CHUNKS) as c:
                for jp in range(2):
                    fetch_routes(c * 2 + jp, jp)
                for u in range(UNITS):
                    act.wait_ge(gate_ready, c * UNITS + u + 1)
                    if u >= 2:
                        act.wait_ge(gated_done, c * UNITS + u - 1)
                    act.activation(tanh[:, u % 2, :], gate_ps[:, u % 2, :], ACT.Tanh, scale=0.5
                                   ).then_inc(tanh_done, 1)
                    if u in EXPS_AFTER:
                        jp = EXPS_AFTER.index(u)
                        route_exps(c * 2 + jp, jp)

        @block.gpsimd
        def _(pool):
            with pool.Fori(0, JT // 2) as pair:
                j0 = pair * 2
                for jp in range(2):
                    pool.wait_ge(scaled, (j0 + jp + 1) * SCALE_STEPS)
                    for h in range(2):
                        row = row_exp[:, jp, h, :].unsqueeze(2).broadcast_to([P, GRID_ROWS, KEYS])
                        col = expo[:, jp, 1, h, :].unsqueeze(1).broadcast_to([P, GRID_ROWS, KEYS])
                        pool.tensor_tensor(grid[:, jp, h, :, :], row, col, ALU.mult).then_inc(grid_done, 1)

        @block.vector
        def _(v):
            def pair_sums(jp, h):
                v.tensor_tensor(sums[:, jp, h, :, :],
                                r[:, jp, 0, h, 0:GRID_ROWS].unsqueeze(2).broadcast_to([P, GRID_ROWS, KEYS]),
                                r[:, jp, 1, h, :].unsqueeze(1).broadcast_to([P, GRID_ROWS, KEYS]),
                                ALU.add).then_inc(scored, 1)

            def score_keys(j, jp):
                v.wait_ge(route_in, j + 1)
                pair_sums(jp, 0)
                for b in range(2):
                    for h in range(2):
                        v.max(best[:, jp, b, h, :], r[:, jp, b, h, :]).then_inc(scored, 1)
                v.wait_ge(scored, j * SCORE_STEPS + 5)
                v.tensor_tensor(pairs[:, jp, :, :, :],
                                best[:, jp, 0, :, :].unsqueeze(3).broadcast_to([P, 2, TOP, TOP]),
                                best[:, jp, 1, :, :].unsqueeze(2).broadcast_to([P, 2, TOP, TOP]),
                                ALU.add).then_inc(scored, 1)
                v.tensor_tensor(below[:, jp, :, :, :].rearrange("p b h k -> p (b h) k"),
                                r[:, jp, :, :, :].rearrange("p b h k -> p (b h) k"),
                                best[:, jp, :, :, 0:1].rearrange("p b h o -> p (b h) o").broadcast_to([P, 4, KEYS]),
                                ALU.subtract).then_inc(scored, 1)

            def score_pairs(j, jp):
                v.wait_ge(scored, j * SCORE_STEPS + 6)
                pair_sums(jp, 1)
                for h in range(2):
                    v.max(top[:, jp, h, :], pairs[:, jp, h, :, :]).then_inc(scored, 1)
                v.wait_ge(scored, j * SCORE_STEPS + 10)
                v.tensor_tensor(top_below[:, jp, :, :], top[:, jp, :, :],
                                top[:, jp, :, 0:1].broadcast_to([P, 2, TOP]), ALU.subtract).then_inc(scored, 1)

            def scale(j, jp):
                v.wait_ge(route_exp, (j + 1) * 2)
                v.reduce_sum(total[:, jp, :], top_exp[:, jp, :, :], axis=AXIS_X).then_inc(scaled, 1)
                v.wait_ge(scaled, j * SCALE_STEPS + 1)
                v.reciprocal(inverse[:, jp, :], total[:, jp, :]).then_inc(scaled, 1)
                v.wait_ge(scaled, j * SCALE_STEPS + 2)
                v.tensor_tensor(row_exp[:, jp, :, :], expo[:, jp, 0, :, 0:GRID_ROWS],
                                inverse[:, jp, :].unsqueeze(2).broadcast_to([P, 2, GRID_ROWS]),
                                ALU.mult).then_inc(scaled, 1)

            def blend(j, jp):
                v.wait_ge(grid_done, (j + 1) * 2)
                v.wait_ge(scored, (j + 1) * SCORE_STEPS)
                for h in range(2):
                    v.scalar_tensor_tensor(out=mix[:, jp, h, :],
                                           in0=sums[:, jp, h, :, :].rearrange("p a b -> p (a b)"),
                                           scalar=top[:, jp, h, TOP - 1:TOP],
                                           in1=grid[:, jp, h, :, :].rearrange("p a b -> p (a b)"),
                                           op0=ALU.is_ge, op1=ALU.mult,
                                           accum_out=inside[:, jp, h:h + 1]).then_inc(mixed, 1)
                v.wait_ge(mixed, j * MIX_STEPS + 2)
                v.tensor_scalar(clipped[:, jp, :], inside[:, jp, :], -1.0, 1.0, ALU.mult, ALU.add).then_inc(mixed, 1)
                v.wait_ge(mixed, j * MIX_STEPS + 3)
                v.tensor_tensor(mix[:, jp, :, EXPERTS - 1], mix[:, jp, :, EXPERTS - 1], clipped[:, jp, :],
                                ALU.add).then_inc(mixed, 1)

            def gate_unit(c, u):
                v.wait_ge(tanh_done, c * UNITS + u + 1)
                v.scalar_tensor_tensor(out=gated[:, u % 2, :], in0=tanh[:, u % 2, :], scalar=1.0,
                                       in1=gate_ps[:, u % 2, :], op0=ALU.add, op1=ALU.mult).then_inc(gated_done, 1)
                v.wait_ge(gated_done, c * UNITS + u + 1)

            def update(c, tt):
                v.wait_ge(out_ready, c * CT + tt + 1)
                v.scalar_tensor_tensor(out=x_sb[:, c * CT + tt, :], in0=out_ps[:, tt % 2, 0:DIM], scalar=0.25,
                                       in1=x_sb[:, c * CT + tt, :], op0=ALU.mult, op1=ALU.add
                                       ).then_inc(x_updated, 1)
                if not store:
                    v.wait_ge(x_updated, c * CT + tt + 1)
                    v.bn_stats(keep["stats"][:, c * CT + tt, :], x_sb[:, c * CT + tt, :]
                               ).then_inc(keep["stats_done"], 1)

            with v.Fori(0, CHUNKS) as c:
                for u in range(FT):
                    gate_unit(c, u)
                    v.wait_ge(up_ready, c * FT + u + 1)
                    v.tensor_tensor(hidden[:, u, :], gated[:, u % 2, :], up_ps[:, u % 2, :],
                                    ALU.mult).then_inc(hidden_done, 1)
                    if u < 4:
                        jp = u // 2
                        if u % 2 == 0:
                            score_keys(c * 2 + jp, jp)
                        else:
                            score_pairs(c * 2 + jp, jp)
                    elif u < 6:
                        scale(c * 2 + u - 4, u - 4)
                    else:
                        blend(c * 2 + u - 6, u - 6)
                for e in range(ET):
                    gate_unit(c, FT + e)
                    v.wait_ge(mix_turned, c * ET + e + 1)
                    v.tensor_tensor(hidden[:, FT + e, :].rearrange("p (j i h) -> p j i h", j=2, h=2),
                                    gated[:, (FT + e) % 2, :].rearrange("p (j i h) -> p j i h", j=2, h=2),
                                    mix_ps[:, e % 2, :].rearrange("p (j h i) -> p j i h", j=2, h=2),
                                    ALU.mult).then_inc(hidden_done, 1)
                for tt in range(CT):
                    update(c, tt)

        @block.sync
        def _(sp):
            if store:
                out_tiles = dram["out"].rearrange("(t p) d -> p t d", p=P)
                with sp.Fori(0, CHUNKS) as c:
                    sp.wait_ge(x_updated, (c + 1) * CT)
                    sp.dma_start(out_tiles[:, ds(c * CT, CT), :], x_sb[:, ds(c * CT, CT), :]).then_inc(stored, 16)
                sp.wait_ge(stored, CHUNKS * 16)


def project_block(nc, sem, dram, keep, attn):
    x_sb, ident = keep["x"], keep["ident"]
    with ExitStack() as scope:
        def sb(n, shape, dt):
            return scope.enter_context(nc.sbuf_tensor(f"proj_{n}", shape, dt))

        def psum(n, shape, dt):
            return scope.enter_context(nc.psum_tensor(f"proj_{n}", shape, dt))

        wide = ("q", "k")
        w_hi = {p: sb(f"w{p}_hi", [P, KT, DIM], F32R) for p in wide}
        w_lo = {p: sb(f"w{p}_lo", [P, KT, DIM], F32R) for p in wide}
        w_v = sb("wv", [P, KT, DIM], F32)
        bias_v = sb("bias_v", [P, DIM], F32)
        bias = {p: sb(f"bias_{p}", [P, KT], F32) for p in wide}
        halves = [sb(f"x{part}", [P, KT, BATCH, SEQ], F32R) for part in ("hi", "lo")]
        n = Norm("proj_norm", sb, psum, sem, halves, DIM)
        stage = {p: sb(f"w{p}_stage", [P, KT, DIM], F32) for p in "qkv"}
        whole = {p: sb(f"w{p}_whole", [P, KT, DIM], F32) for p in wide} | {"v": w_v}
        lora_b = {p: sb(f"lora_b{p}", [RANK, DIM], F32) for p in "qkv"}
        lora_a = {p: sb(f"lora_a{p}", [RANK, DIM], F32) for p in "qkv"}
        update_ps = psum("update_ps", [P, 2, KT, DIM], F32)
        qk_ps = psum("qk_ps", [P, 2, CHUNK], F32)

        weights_in = {p: sem(f"proj_w{p}_in") for p in "qkv"}
        bias_in = sem("proj_bias_in")
        update_ready = sem("proj_update_ready")
        whole_done = sem("proj_whole_done")
        w_hi_done, w_lo_done = sem("proj_w_hi_done"), sem("proj_w_lo_done")
        qk_ready = sem("proj_qk_ready")
        qk_hi_done = sem("proj_qk_hi_done")
        qk_lo_done = sem("proj_qk_lo_done")
        block = scope.enter_context(nc.Block())

        @block.sync
        def _(sp):
            for p in "qkv":
                sp.dma_start(stage[p][:, :, :], dram[f"w{p}_t"].rearrange("(k p) o -> p k o", p=P)
                             ).then_inc(weights_in[p], 16)
                sp.dma_start(lora_b[p][:, :], dram[f"lora_b{p}"]).then_inc(weights_in[p], 16)
                sp.dma_start(lora_a[p][:, :], dram[f"lora_a{p}_t"]).then_inc(weights_in[p], 16)
            for p in wide:
                sp.dma_start(bias[p][:, :], dram[f"b{p}_columns"]).then_inc(bias_in, 16)
            sp.dma_start(bias_v[:, :], dram["bv"].partition_broadcast(P)).then_inc(bias_in, 16)

        @block.gpsimd
        def _(pool):
            norm_on_gpsimd(pool, n, keep["minus_half"][:, :])

        @block.tensor
        def _(pe):
            for i, p in enumerate("qkv"):
                pe.wait_ge(weights_in[p], 48)
                if i >= 2:
                    pe.wait_ge(whole_done, i - 1)
                for k in range(KT):
                    update = pe.matmul(update_ps[:, i % 2, k, :], lora_b[p][:, k * P:(k + 1) * P], lora_a[p][:, :],
                                       start=True, stop=True)
                update.then_inc(update_ready, 1)
            pe.wait_ge(whole_done, 3)
            norm_on_tensor(pe, n, ident[:, :], lambda k, b: w_v[:, k, :])
            pe.wait_ge(w_lo_done, len(wide))
            with pe.Fori(0, CHUNKS) as c:
                tokens = n.token_halves(c)
                for i, p in enumerate(wide):
                    for f in range(KT):
                        at = slice(f * P, (f + 1) * P)
                        pe.wait_ge(qk_lo_done, c * 4 + i * KT + f + 1)
                        product3(pe, qk_ps[:, f, :],
                                 [(w_hi[p][:, k, at], w_lo[p][:, k, at]) for k in range(KT)],
                                 tokens).then_inc(qk_ready, 1)

        @block.scalar
        def _(act):
            norm_on_scalar(act, n)
            act.wait_ge(whole_done, len(wide))
            for i, p in enumerate(wide):
                act.activation(w_hi[p][:, :, :], whole[p][:, :, :], ACT.Copy).then_inc(w_hi_done, 1)
            act.wait_ge(bias_in, 48)
            with act.Fori(0, CHUNKS) as c:
                for i, p in enumerate(wide):
                    for f in range(KT):
                        act.wait_ge(qk_ready, c * 4 + i * KT + f + 1)
                        act.activation(attn[f"{p}_hi"][:, f, ds(c * CHUNK, CHUNK)], qk_ps[:, f, :], ACT.Identity,
                                       bias=bias[p][:, f:f + 1]).then_inc(qk_hi_done, 1)

        @block.vector
        def _(v):
            v.sem_inc(n.lo_done, FIRST)
            v.sem_inc(n.rows_out, FIRST)
            v.sem_inc(qk_lo_done, FIRST)
            for i, p in enumerate("qkv"):
                v.wait_ge(update_ready, i + 1)
                v.scalar_tensor_tensor(out=whole[p][:, :, :], in0=update_ps[:, i % 2, :, :], scalar=LORA_SCALE,
                                       in1=stage[p][:, :, :], op0=ALU.mult, op1=ALU.add).then_inc(whole_done, 1)
            v.wait_ge(bias_in, 48)

            def v_rows_out(v, j, par):
                for b in range(BATCH):
                    out = attn["v"][:, :, b, j, :, :]
                    done = v.tensor_tensor(
                        out, n.rows_ps[:, par, b * DIM:(b + 1) * DIM].rearrange("p (f h d) -> p f h d", f=KT, d=HD),
                        bias_v[:, :].rearrange("p (f h d) -> p f h d", f=KT, d=HD), ALU.add)
                done.then_inc(n.rows_out, 1)

            norm_on_vector(v, n, x_sb, keep["stats"], v_rows_out)
            for i, p in enumerate(wide):
                v.wait_ge(w_hi_done, i + 1)
                v.tensor_tensor(w_lo[p][:, :, :], whole[p][:, :, :], w_hi[p][:, :, :].bitcast(F32),
                                ALU.subtract).then_inc(w_lo_done, 1)
            with v.Fori(0, CHUNKS) as c:
                for i, p in enumerate(wide):
                    for f in range(KT):
                        v.wait_ge(qk_hi_done, c * 4 + i * KT + f + 1)
                        at = ds(c * CHUNK, CHUNK)
                        v.scalar_tensor_tensor(out=attn[f"{p}_lo"][:, f, at], in0=qk_ps[:, f, :],
                                               scalar=bias[p][:, f:f + 1], in1=attn[f"{p}_hi"][:, f, at].bitcast(F32),
                                               op0=ALU.add, op1=ALU.subtract).then_inc(qk_lo_done, 1)


def attention_block(nc, sem, attn):
    SLOTS, HALF = 4, SEQ // 2
    ITS = KT * BATCH
    KEY_TILES = SEQ // P
    STRIP = 32
    ROWS = 4 * HD
    MAXES = 2 * KEY_TILES * 2
    STACK_DMAS = 17
    SCORES = KEY_TILES * 2 * 2
    EARLY = 14
    TURN_AT = 5
    RING = 3
    assert MAXES % RING == SCORES % RING == 2
    last_reader = lambda i: (i if i >= RING else (1, 2, 0)[i]) + 1
    with ExitStack() as scope:
        def sb(n, shape, dt):
            return scope.enter_context(nc.sbuf_tensor(n, shape, dt))

        def psum(n, shape, dt):
            return scope.enter_context(nc.psum_tensor(n, shape, dt))

        q_stack = [sb(f"q_stack{s}", [P, 2, SEQ], F32R) for s in range(SLOTS)]
        k_stack = [sb(f"k_stack{s}", [P, 2, SEQ], F32R) for s in range(SLOTS)]
        values = [sb(f"values{s}", [P, KEY_TILES, 2, STRIP], F32) for s in range(SLOTS)]
        probs = sb("probs", [P, 2, 2, SEQ], F32)
        maxima = sb("maxima", [P, 2, MAXES // 2, 2], F32)
        maximum = sb("maximum", [P, 2, MAXES // 2], F32)
        max_rows = sb("max_rows", [MAXES // 2, 2, P], F32R)
        mixed = sb("mixed_t", [P, HALF], F32)
        inverse = sb("inverse_sum", [P, KEY_TILES // 2, 4], F32)
        score_ps = psum("score_ps", [P, RING, HALF], F32)
        max_ps = psum("max_ps", [P, RING, HALF], F32)
        mixed_ps = psum("mixed_ps", [P, HALF], F32)
        turn_ps = psum("turn_ps", [P, KEY_TILES // 2, 4, STRIP], F32)

        stacks_in = [sem(f"stacks_in{s}") for s in range(SLOTS)]
        max_in = [sem(f"max_in{s}") for s in range(SLOTS)]
        q_cleared = sem("q_cleared")
        ones_set = sem("ones_set")
        values_in = sem("values_in")
        early_scored = sem("early_scored")
        early_max = sem("early_max")
        tile_scored = sem("tile_scored")
        tile_max = sem("tile_max")
        group_max = sem("group_max")
        max_turned = sem("max_turned")
        max_negated = sem("max_negated")
        scores_ready = sem("scores_ready")
        probs_ready = sem("probs_ready")
        probs_used = sem("probs_used")
        mixed_out = sem("mixed_out")
        mixed_turned = [sem(f"mixed_turned{s}") for s in range(SLOTS)]
        inverted = sem("inverted")
        group_out = sem("group_out")
        block = scope.enter_context(nc.Block())

        @block.sync
        def _(sp):
            def load_stacks(it, s):
                for stack, parts in ((q_stack[s], ("q_hi", "q_hi", "q_lo", "q_lo")),
                                     (k_stack[s], ("k_hi", "k_lo", "k_hi", "k_lo"))):
                    for i, part in enumerate(parts):
                        source = attn[part][:, :, :].rearrange("p f n -> p (f n)")
                        for j in range(2):
                            at = s * 2 * HD + j * HD
                            sp.dma_start(stack[i * HD:(i + 1) * HD, j, :].bitcast(F32),
                                         source[at:at + HD, ds(it * SEQ, SEQ)].bitcast(F32)
                                         ).then_inc(stacks_in[s], 16)
                sp.dma_start(q_stack[s][ROWS:ROWS + 1, :, :].bitcast(F32),
                             q_stack[s][ROWS + 1:ROWS + 2, :, :].bitcast(F32)).then_inc(stacks_in[s], 16)

            def load_maxima(count, par, s):
                sp.wait_ge(max_negated, count)
                sp.dma_start(q_stack[s][ROWS:ROWS + 1, :, :].rearrange("o j (t q) -> o (j t) q", q=P).bitcast(F32),
                             max_rows[:, par, :].bitcast(F32)).then_inc(max_in[s], 16)

            for s in range(SLOTS):
                sp.wait_ge(q_cleared, s + 1)
                load_stacks(0, s)
            load_maxima(1, 0, 0)
            with sp.Fori(0, ITS - 1) as it:
                for s in range(SLOTS):
                    load_maxima(it * SLOTS + s + 2, (s + 1) % 2, (s + 1) % SLOTS)
                    sp.wait_ge(mixed_turned[s], it + 2)
                    load_stacks(it + 1, s)
            for s in range(SLOTS - 1):
                load_maxima((ITS - 1) * SLOTS + s + 2, (s + 1) % 2, s + 1)

        @block.gpsimd
        def _(pool):
            for s in range(SLOTS):
                pool.memset(k_stack[s][ROWS:P, :, :].bitcast(F32), 0.0).then_inc(ones_set, 1)
                pool.wait_ge(ones_set, 4 * s + 1)
                pool.memset(k_stack[s][ROWS:ROWS + 1, :, :].bitcast(F32), 1.0).then_inc(ones_set, 1)
                pool.wait_ge(ones_set, 4 * s + 2)
                pool.memset(values[s][:, :, :, :], 0.0).then_inc(ones_set, 1)
                pool.wait_ge(ones_set, 4 * s + 3)
                pool.memset(values[s][:, :, :, HD:HD + 1], 1.0).then_inc(ones_set, 1)
                pool.wait_ge(ones_set, 4 * s + 4)
            by_group = attn["v"][:, :, :, :, :, :].rearrange("p f b j h d -> p (f b) j (h d)")
            with pool.Fori(0, ITS) as it:
                for s in range(SLOTS):
                    pool.wait_ge(mixed_turned[s], it + 1)
                    pool.tensor_copy(values[s][:, :, :, 0:HD],
                                     by_group[:, it, :, s * 2 * HD:(s + 1) * 2 * HD]
                                     .rearrange("p j (h d) -> p j h d", d=HD)).then_inc(values_in, 1)

        @block.tensor
        def _(pe):
            ident = attn["ident"]

            def max_scores(group, s, i, scored, taken):
                j, qt, half = i // 16, i // 2 % KEY_TILES, i % 2
                pe.wait_ge(taken, group * MAXES + last_reader(i))
                pe.matmul(max_ps[:, i % RING, :], q_stack[s][:, j, qt * P:(qt + 1) * P],
                          k_stack[s][:, j, half * HALF:(half + 1) * HALF], start=True, stop=True
                          ).then_inc(scored, 1)

            def turn_group_max(count, par, groups_out):
                pe.wait_ge(group_max, count)
                pe.wait_ge(group_out, groups_out + 1)
                pe.transpose(turn_ps[0:MAXES // 2, :, :, :].rearrange("p a b c -> p (a b c)")[:, 0:P],
                             maximum[:, par, :], ident).then_inc(max_turned, 1)

            def score(group, s, i):
                kt, j, half = i // 4, i // 2 % 2, i % 2
                pe.wait_ge(probs_ready, group * SCORES + last_reader(i))
                pe.matmul(score_ps[:, i % RING, :], k_stack[s][:, j, kt * P:(kt + 1) * P],
                          q_stack[s][:, j, half * HALF:(half + 1) * HALF], start=True, stop=True
                          ).then_inc(scores_ready, 1)

            def slot(it, s, last):
                group = it * SLOTS + s
                next_slot, next_it = (s + 1) % SLOTS, it + (s + 1) // SLOTS
                has_next = not (last and s + 1 >= SLOTS)

                def ahead(step):
                    i, later = (step + EARLY) % MAXES, (step + EARLY) // MAXES
                    if not (last and s + 1 + later >= SLOTS):
                        if i == 0:
                            pe.wait_ge(stacks_in[(s + 2) % SLOTS], (it + (s + 2) // SLOTS + 1) * STACK_DMAS * 16)
                        max_scores(group + later, (s + 1 + later) % SLOTS, i, tile_scored, tile_max)

                def mix(kt):
                    pe.wait_ge(probs_ready, group * SCORES + kt * 4 + 4 + RING)
                    if kt == 0:
                        pe.wait_ge(mixed_out, group + 1)
                        pe.wait_ge(values_in, group + 1)
                    for j in range(2):
                        for half in range(2):
                            strip = (j * 2 + half) * STRIP
                            mm = pe.matmul(mixed_ps[strip:strip + STRIP, :], values[s][:, kt, j, :],
                                           probs[:, kt % 2, j, half * HALF:(half + 1) * HALF],
                                           start=(kt == 0), stop=(kt == KEY_TILES - 1),
                                           tile_position=(0, strip))
                    mm.then_inc(probs_used, 1)

                for kt in range(1, KEY_TILES):
                    for i in range(4):
                        score(group, s, 4 * kt + i)
                        if i == 3:
                            mix(kt - 1)
                        ahead(4 * (kt - 1) + i)
                    if kt == TURN_AT and has_next:
                        turn_group_max(group + 2, (s + 1) % 2, group * 2)
                for i in range(4):
                    if i == 2:
                        mix(KEY_TILES - 1)
                    ahead(MAXES - 4 + i)
                    if has_next:
                        if i == 0:
                            pe.wait_ge(max_in[next_slot], (next_it + 1) * 16)
                        score(group + 1, next_slot, i)
                pe.wait_ge(mixed_out, group + 2)
                if has_next:
                    pe.wait_ge(max_negated, group + 2)
                else:
                    pe.wait_ge(group_out, group * 2 + 1)
                for qt in range(KEY_TILES // 2):
                    turn = pe.transpose(turn_ps[:, qt, :, :].rearrange("p a b -> p (a b)"),
                                        mixed[:, qt * P:(qt + 1) * P], ident)
                turn.then_inc(mixed_turned[s], 1)

            for s in range(SLOTS):
                pe.sem_inc(mixed_turned[s], 1)
            pe.wait_ge(ones_set, 2)
            pe.wait_ge(stacks_in[0], STACK_DMAS * 16)
            for i in range(MAXES):
                max_scores(0, 0, i, early_scored, early_max)
            pe.wait_ge(early_max, MAXES + RING)
            pe.wait_ge(ones_set, 4 * SLOTS)
            pe.wait_ge(stacks_in[1], STACK_DMAS * 16)
            for i in range(EARLY):
                max_scores(0, 1, i, tile_scored, tile_max)
                if i == 2:
                    turn_group_max(1, 0, 0)
            pe.wait_ge(max_in[0], 16)
            for i in range(4):
                score(0, 0, i)
            with pe.Fori(0, ITS - 1) as it:
                for s in range(SLOTS):
                    slot(it, s, False)
            for s in range(SLOTS):
                slot(ITS - 1, s, True)

        @block.scalar
        def _(act):
            def negate_maxima(count, par):
                act.wait_ge(max_turned, count)
                act.activation(max_rows[:, par, :],
                               turn_ps[0:MAXES // 2, :, :, :].rearrange("p a b c -> p (a b c)")[:, 0:P],
                               ACT.Copy, scale=-1.0).then_inc(max_negated, 1)

            def exponentials(group, indices):
                for i in indices:
                    kt, j, half = i // 4, i // 2 % 2, i % 2
                    act.wait_ge(scores_ready, group * SCORES + i + 1)
                    act.activation(probs[:, kt % 2, j, half * HALF:(half + 1) * HALF], score_ps[:, i % RING, :],
                                   ACT.Exp, scale=SCORE_SCALE).then_inc(probs_ready, 1)

            def slot(it, s, last):
                group = it * SLOTS + s
                has_next = not (last and s + 1 >= SLOTS)
                for kt in range(1, KEY_TILES):
                    if kt >= 2:
                        act.wait_ge(probs_used, group * KEY_TILES + kt - 1)
                    exponentials(group, range(4 * kt, 4 * kt + 4))
                    if kt == TURN_AT and has_next:
                        negate_maxima(group + 2, (s + 1) % 2)
                if has_next:
                    act.wait_ge(probs_used, group * KEY_TILES + KEY_TILES - 1)
                    exponentials(group + 1, (0, 1))
                act.wait_ge(probs_used, (group + 1) * KEY_TILES)
                act.activation(mixed[:, :], mixed_ps[:, :], ACT.Copy).then_inc(mixed_out, 1)
                if has_next:
                    exponentials(group + 1, (2, 3))

            act.sem_inc(mixed_out, 1)
            act.sem_inc(probs_ready, RING)
            negate_maxima(1, 0)
            exponentials(0, range(4))
            with act.Fori(0, ITS - 1) as it:
                for s in range(SLOTS):
                    slot(it, s, False)
            for s in range(SLOTS):
                slot(ITS - 1, s, True)

        @block.vector
        def _(v):
            def take_maxima(group, par, scored, taken, indices=range(MAXES)):
                for i in indices:
                    v.wait_ge(scored, group * MAXES + i + 1)
                    v.reduce_max(maxima[:, par, i // 2, i % 2:i % 2 + 1], max_ps[:, i % RING, :], axis=AXIS_X
                                 ).then_inc(taken, 1)

            def close_maxima(group, par, taken):
                v.wait_ge(taken, (group + 1) * MAXES + RING)
                v.tensor_tensor(maximum[:, par, :], maxima[:, par, :, 0], maxima[:, par, :, 1], ALU.max
                                ).then_inc(group_max, 1)

            def write_out(it, s):
                group = it * SLOTS + s
                v.wait_ge(mixed_turned[s], it + 2)
                v.reciprocal(inverse[:, :, :], turn_ps[:, :, :, HD]).then_inc(inverted, 1)
                v.wait_ge(inverted, group + 1)
                for j in range(2):
                    at = s * 2 * HD + j * HD
                    v.tensor_tensor(
                        attn["out"][:, it, :, at:at + HD].rearrange("p (half t) d -> p half t d", half=2),
                        turn_ps[:, :, 2 * j:2 * j + 2, 0:HD].rearrange("p t half d -> p half t d"),
                        inverse[:, :, 2 * j:2 * j + 2].rearrange("p t half -> p half t").unsqueeze(3)
                        .broadcast_to([P, 2, KEY_TILES // 2, HD]),
                        ALU.mult).then_inc(group_out, 1)

            def slot(it, s, last):
                group = it * SLOTS + s
                if not (last and s + 1 >= SLOTS):
                    take_maxima(group, (s + 1) % 2, tile_scored, tile_max, range(EARLY, MAXES))
                    close_maxima(group, (s + 1) % 2, tile_max)
                if not (last and s + 2 >= SLOTS):
                    take_maxima(group + 1, s % 2, tile_scored, tile_max, range(EARLY))
                write_out(it, s)

            v.sem_inc(group_out, 1)
            v.sem_inc(early_max, RING)
            v.sem_inc(tile_max, RING)
            for s in range(SLOTS):
                v.memset(q_stack[s][ROWS:P, :, :].bitcast(F32), 0.0).then_inc(q_cleared, 1)
            take_maxima(0, 0, early_scored, early_max)
            close_maxima(0, 0, early_max)
            take_maxima(0, 1, tile_scored, tile_max, range(EARLY))
            with v.Fori(0, ITS - 1) as it:
                for s in range(SLOTS):
                    slot(it, s, False)
            for s in range(SLOTS):
                slot(ITS - 1, s, True)


def output_block(nc, sem, dram, keep, attn):
    x_sb, ident = keep["x"], keep["ident"]
    with ExitStack() as scope:
        def sb(n, shape, dt):
            return scope.enter_context(nc.sbuf_tensor(f"o_{n}", shape, dt))

        def psum(n, shape, dt):
            return scope.enter_context(nc.psum_tensor(f"o_{n}", shape, dt))

        stage = sb("stage", [P, KT, DIM], F32)
        w_o = sb("w", [P, KT, DIM], F32)
        bias_o = sb("bias", [P, DIM], F32)
        lora_b, lora_a = sb("lora_b", [RANK, DIM], F32), sb("lora_a", [RANK, DIM], F32)
        rows = sb("rows", [P, 2, DIM], F32)
        columns = sb("columns", [P, 2, KT, P], F32)
        biased = sb("biased", [P, 2, DIM], F32)
        update_ps = psum("update_ps", [P, 2, DIM], F32)
        columns_ps = psum("columns_ps", [P, 2, 512], F32)
        out_ps = psum("out_ps", [P, 2, 512], F32)

        weights_in, bias_in = sem("o_weights_in"), sem("o_bias_in")
        update_ready, whole_done = sem("o_update_ready"), sem("o_whole_done")
        rows_done = sem("o_rows_done")
        turned = sem("o_turned")
        columns_done = sem("o_columns_done")
        out_ready = sem("o_out_ready")
        biased_done = sem("o_biased_done")
        x_updated = sem("o_x_updated")
        block = scope.enter_context(nc.Block())

        @block.sync
        def _(sp):
            sp.dma_start(stage[:, :, :], dram["wo_t"].rearrange("(k p) o -> p k o", p=P)).then_inc(weights_in, 16)
            sp.dma_start(lora_b[:, :], dram["lora_bo"]).then_inc(weights_in, 16)
            sp.dma_start(lora_a[:, :], dram["lora_ao_t"]).then_inc(weights_in, 16)
            sp.dma_start(bias_o[:, :], dram["bo"].partition_broadcast(P)).then_inc(bias_in, 16)

        @block.tensor
        def _(pe):
            pe.sem_inc(turned, FIRST)
            pe.sem_inc(out_ready, FIRST)
            pe.wait_ge(weights_in, 48)
            for k in range(KT):
                update = pe.matmul(update_ps[:, k, :], lora_b[:, k * P:(k + 1) * P], lora_a[:, :],
                                   start=True, stop=True)
            update.then_inc(update_ready, 1)
            pe.wait_ge(whole_done, 1)
            with pe.Fori(0, TILES // 2) as pair:
                for par in range(2):
                    t = pair * 2 + par
                    pe.wait_ge(rows_done, t + 1)
                    pe.wait_ge(columns_done, t + 1)
                    for k in range(KT):
                        turn = pe.transpose(columns_ps[:, par, k * P:(k + 1) * P], rows[:, par, k * P:(k + 1) * P],
                                            ident[:, :])
                    turn.then_inc(turned, 1)
                for par in range(2):
                    t = pair * 2 + par
                    pe.wait_ge(columns_done, t + 1 + FIRST)
                    pe.wait_ge(x_updated, t + 1)
                    for k in range(KT):
                        out = pe.matmul(out_ps[:, par, 0:DIM], columns[:, par, k, :], w_o[:, k, :],
                                        start=(k == 0), stop=(k == KT - 1))
                    out.then_inc(out_ready, 1)

        @block.scalar
        def _(act):
            act.sem_inc(columns_done, FIRST)
            by_tile = attn["out"][:, :, :, :].rearrange("p (f b) j d -> p f (b j) d", f=KT)
            with act.Fori(0, TILES // 2) as pair:
                for par in range(2):
                    t = pair * 2 + par
                    act.wait_ge(turned, t + 1)
                    act.activation(rows[:, par, :].rearrange("p (f d) -> p f d", f=KT), by_tile[:, :, t, :],
                                   ACT.Copy).then_inc(rows_done, 1)
                for par in range(2):
                    t = pair * 2 + par
                    act.wait_ge(turned, t + 1 + FIRST)
                    act.wait_ge(out_ready, t + 1)
                    act.activation(columns[:, par, :, :].rearrange("p k q -> p (k q)"), columns_ps[:, par, 0:DIM],
                                   ACT.Copy).then_inc(columns_done, 1)

        @block.vector
        def _(v):
            v.sem_inc(x_updated, FIRST)
            v.wait_ge(update_ready, 1)
            v.scalar_tensor_tensor(out=w_o[:, :, :], in0=update_ps[:, :, :], scalar=LORA_SCALE,
                                   in1=stage[:, :, :], op0=ALU.mult, op1=ALU.add).then_inc(whole_done, 1)
            v.wait_ge(bias_in, 16)
            with v.Fori(0, TILES // 2) as pair:
                for par in range(2):
                    t = pair * 2 + par
                    v.wait_ge(x_updated, t + 1)
                    v.tensor_tensor(biased[:, par, :], x_sb[:, t, :], bias_o[:, :], ALU.add).then_inc(biased_done, 1)
                for par in range(2):
                    t = pair * 2 + par
                    v.wait_ge(biased_done, t + 1)
                    v.wait_ge(out_ready, t + 1 + FIRST)
                    v.tensor_tensor(x_sb[:, t, :], out_ps[:, par, 0:DIM], biased[:, par, :], ALU.add
                                    ).then_inc(x_updated, 1)
                for par in range(2):
                    t = pair * 2 + par
                    v.wait_ge(x_updated, t + 1 + FIRST)
                    v.bn_stats(keep["stats"][:, t, :], x_sb[:, t, :]).then_inc(keep["stats_done"], 1)


def attention(nc, sem, dram, keep):
    with ExitStack() as scope:
        def sb(name, shape, dt):
            return scope.enter_context(nc.sbuf_tensor(name, shape, dt))

        attn = {"ident": keep["ident"][:, :], "out": sb("attn_out", [P, KT * BATCH, JT, P], F32)}
        with ExitStack() as inner:
            for part in ("q_hi", "q_lo", "k_hi", "k_lo"):
                attn[part] = inner.enter_context(nc.sbuf_tensor(part, [P, KT, TOKENS], F32R))
            attn["v"] = inner.enter_context(nc.sbuf_tensor("v_rows", [P, KT, BATCH, JT, HEADS // KT, HD], F32))
            project_block(nc, sem, dram, keep, attn)
            attention_block(nc, sem, attn)
        output_block(nc, sem, dram, keep, attn)


def macaron(nc, dram):
    with ExitStack() as outer:
        def sb(name, shape, dt):
            return outer.enter_context(nc.sbuf_tensor(name, shape, dt))

        def sem(name):
            return outer.enter_context(nc.semaphore(name))

        keep = {
            "x": sb("x_sb", [P, TILES, DIM], F32),
            "ident": sb("ident", [P, P], F32),
            "minus_half": sb("minus_half", [P, TILES], F32),
            "route_w": sb("route_w", [P, KT, 2, 2, KEYS], F32),
            "stats": sb("stats", [P, TILES, 6], F32),
            "stats_done": sem("stats_done"),
            "ident_done": sem("ident_done"),
        }
        setup_block(nc, outer, sem, dram, keep)
        ffn_block(nc, sem, dram, keep, 0)
        attention(nc, sem, dram, keep)
        ffn_block(nc, sem, dram, keep, 1)


def kernel(L0_attn_x, L0_attn_Wq, L0_attn_bq, L0_attn_Bq, L0_attn_Aq, L0_attn_Wk, L0_attn_bk, L0_attn_Bk,
           L0_attn_Ak, L0_attn_Wv, L0_attn_bv, L0_attn_Bv, L0_attn_Av, L0_attn_Wo, L0_attn_bo, L0_attn_Bo,
           L0_attn_Ao, L0_ffn_W_q, L0_ffn_keys, L0_ffn_down_embed, L0_ffn_up_embed, L0_ffn_gate_w,
           L0_ffn_up_w, L0_ffn_down_w):
    import numpy as np
    import concourse.bacc as bacc
    from concourse.bass_utils import run_bass_kernel_spmd

    nc = bacc.Bacc("TRN2", target_bir_lowering=False, num_devices=1)
    laid = {
        "x": np.asarray(L0_attn_x).reshape(TOKENS, DIM),
        "retrieval_t": np.asarray(L0_ffn_W_q).T, "keys": L0_ffn_keys,
        "gate": L0_ffn_gate_w, "up": L0_ffn_up_w, "down": L0_ffn_down_w,
        "down_embed": np.asarray(L0_ffn_down_embed).T, "up_embed": L0_ffn_up_embed,
    }
    for p, (w, b, bm, am) in {"q": (L0_attn_Wq, L0_attn_bq, L0_attn_Bq, L0_attn_Aq),
                              "k": (L0_attn_Wk, L0_attn_bk, L0_attn_Bk, L0_attn_Ak),
                              "v": (L0_attn_Wv, L0_attn_bv, L0_attn_Bv, L0_attn_Av),
                              "o": (L0_attn_Wo, L0_attn_bo, L0_attn_Bo, L0_attn_Ao)}.items():
        laid |= {f"w{p}_t": np.asarray(w).T, f"b{p}": b, f"lora_b{p}": bm, f"lora_a{p}_t": np.asarray(am).T}
        if p in "qk":
            laid[f"b{p}_columns"] = np.asarray(b).reshape(KT, P).T
    arrays, dram = {}, {}
    for name, a in laid.items():
        arrays[f"in_{name}"] = a = np.ascontiguousarray(a)
        dram[name] = nc.dram_tensor(f"in_{name}", a.shape, mybir.dt.from_np(a.dtype), kind="ExternalInput").ap()
    dram["out"] = nc.dram_tensor("out", (TOKENS, DIM), F32, kind="ExternalOutput").ap()
    macaron(nc, dram)
    r = run_bass_kernel_spmd(nc, [arrays], core_ids=[0])
    return np.asarray(r.results[0]["out"]).reshape(BATCH, SEQ, DIM)
```

```python
from contextlib import ExitStack

import concourse.bass as bass
from concourse import mybir

F32 = mybir.dt.float32
F32R = mybir.dt.float32r
ALU = mybir.AluOpType
ACT = mybir.ActivationFunctionType
AXIS_X = mybir.AxisListType.X
ds = bass.ds

P = 128
BATCH, SEQ, DIM = 2, 1024, 256
TOKENS = BATCH * SEQ
KT = DIM // P
TILES = TOKENS // P
JT = SEQ // P
CHUNK = 512
CHUNKS = TOKENS // CHUNK
CT = CHUNK // P
HEADS, HD, RANK = 16, 16, 16
LORA_SCALE = 8.0 / RANK
SCORE_SCALE = HD ** -0.5
INTER, EXPERTS, KEYS, RETRIEVAL, TOP = 1024, 512, 64, 128, 8
GRID_ROWS = EXPERTS // KEYS
FT = INTER // P
ET = EXPERTS // P
UNITS = FT + ET
EPS = 1e-5
FIRST = 2


def product3(pe, out, w, x):
    last = len(w) - 1
    for k, ((w_hi, w_lo), (x_hi, x_lo)) in enumerate(zip(w, x)):
        pe.matmul(out, w_hi, x_hi, start=(k == 0), stop=False)
        pe.matmul(out, w_lo, x_hi, start=False, stop=False)
        done = pe.matmul(out, w_hi, x_lo, start=False, stop=(k == last))
    return done


class Norm:

    def __init__(self, name, sb, psum, sem, halves, rows_width):
        self.xhi, self.xlo = halves
        self.work = sb(f"{name}_work", [P, 4, TILES], F32)
        self.mean = sb(f"{name}_mean", [P, TILES], F32)
        self.var = sb(f"{name}_var", [P, TILES], F32)
        self.rstd = sb(f"{name}_rstd", [P, TILES], F32)
        self.xn = sb(f"{name}_xn", [P, 2, BATCH, DIM], F32)
        self.full = sb(f"{name}_full", [P, 2, KT, BATCH, P], F32)
        self.turned_ps = psum(f"{name}_turned", [P, 2, KT, BATCH, P], F32)
        self.rows_ps = psum(f"{name}_rows", [P, 2, 512], F32)
        self.rows_width = rows_width
        self.var_done = sem(f"{name}_var_done")
        self.rstd_done = sem(f"{name}_rstd_done")
        self.xn_done = sem(f"{name}_xn_done")
        self.turned = sem(f"{name}_turned_done")
        self.full_done = sem(f"{name}_full_done")
        self.hi_done = sem(f"{name}_hi_done")
        self.lo_done = sem(f"{name}_lo_done")
        self.rows_done = sem(f"{name}_rows_done")
        self.rows_out = sem(f"{name}_rows_out")

    def token_halves(self, c):
        hi = self.xhi[:, :, :, :].rearrange("p k b s -> p k (b s)")
        lo = self.xlo[:, :, :, :].rearrange("p k b s -> p k (b s)")
        return [(hi[:, k, ds(c * CHUNK, CHUNK)], lo[:, k, ds(c * CHUNK, CHUNK)]) for k in range(KT)]


def variances_on_vector(v, n, stats):
    even_mean, odd_mean = stats[:, :, 1], stats[:, :, 4]
    even_m2, odd_m2 = stats[:, :, 2], stats[:, :, 5]
    v.tensor_tensor(n.work[:, 0, :], even_mean, odd_mean, ALU.add).then_inc(n.var_done, 1)
    v.tensor_tensor(n.work[:, 1, :], even_mean, odd_mean, ALU.subtract).then_inc(n.var_done, 1)
    v.tensor_tensor(n.work[:, 2, :], even_m2, odd_m2, ALU.add).then_inc(n.var_done, 1)
    v.wait_ge(n.var_done, 3)
    v.tensor_scalar(n.mean[:, :], n.work[:, 0, :], 0.5, None, ALU.mult).then_inc(n.var_done, 1)
    v.tensor_tensor(n.work[:, 3, :], n.work[:, 1, :], n.work[:, 1, :], ALU.mult).then_inc(n.var_done, 1)
    v.wait_ge(n.var_done, 5)
    v.tensor_scalar(n.work[:, 0, :], n.work[:, 3, :], 0.25, EPS, ALU.mult, ALU.add).then_inc(n.var_done, 1)
    v.wait_ge(n.var_done, 6)
    v.scalar_tensor_tensor(out=n.var[:, :], in0=n.work[:, 2, :], scalar=1.0 / DIM, in1=n.work[:, 0, :],
                           op0=ALU.mult, op1=ALU.add).then_inc(n.var_done, 1)


def norm_on_vector(v, n, x_sb, rows_evacuation=None, beside=None):
    def normalize(j, par, pair):
        v.wait_ge(n.rstd_done, pair + 1)
        v.wait_ge(n.turned, j + 1)
        for b in range(BATCH):
            t = b * JT + j
            v.tensor_scalar(n.xn[:, par, b, :], x_sb[:, t, :], n.mean[:, ds(t, 1)], n.rstd[:, ds(t, 1)],
                            ALU.subtract, ALU.mult).then_inc(n.xn_done, 1)

    def low_parts(j, par):
        at = ds(j * P, P)
        v.wait_ge(n.hi_done, j + 1)
        v.tensor_tensor(n.xlo[:, :, :, at], n.turned_ps[:, par, :, :, :], n.xhi[:, :, :, at].bitcast(F32),
                        ALU.subtract).then_inc(n.lo_done, 1)

    def rows_out(j, par):
        if rows_evacuation is not None:
            v.wait_ge(n.rows_done, j + 1 + FIRST)
            rows_evacuation(v, j, par)

    normalize(0, 0, 0)
    normalize(1, 1, 0)
    with v.Fori(0, JT // 2 - 1) as pair:
        for par in range(2):
            j = pair * 2 + par
            low_parts(j, par)
            normalize(j + 2, par, pair + 1)
            rows_out(j, par)
            if par == 0 and beside is not None:
                beside(j)
    for par in range(2):
        low_parts(JT - 2 + par, par)
        rows_out(JT - 2 + par, par)
        if par == 0 and beside is not None:
            beside(JT - 2)


def norm_on_gpsimd(pool, n, minus_half):
    pool.wait_ge(n.var_done, 7)
    rstd, var, power = (a.rearrange("p (b j) -> p b j", b=BATCH) for a in (n.rstd[:, :], n.var[:, :], minus_half))
    for j in range(0, JT, 2):
        pool.tensor_tensor(rstd[:, :, j:j + 2], var[:, :, j:j + 2], power[:, :, j:j + 2], ALU.pow
                           ).then_inc(n.rstd_done, 1)


def norm_on_tensor(pe, n, ident, rows_weights):
    pe.sem_inc(n.turned, FIRST)
    pe.sem_inc(n.rows_done, FIRST)

    def turn(j, par):
        pe.wait_ge(n.xn_done, (j + 1) * BATCH)
        pe.wait_ge(n.lo_done, j + 1)
        for k in range(KT):
            for b in range(BATCH):
                turned = pe.transpose(n.turned_ps[:, par, k, b, :], n.xn[:, par, b, k * P:(k + 1) * P], ident)
        turned.then_inc(n.turned, 1)

    def rows_product(j, par):
        pe.wait_ge(n.full_done, j + 1)
        pe.wait_ge(n.rows_out, j + 1)
        w = n.rows_width
        for b in range(BATCH):
            for k in range(KT):
                rows = pe.matmul(n.rows_ps[:, par, b * w:(b + 1) * w], n.full[:, par, k, b, :],
                                 rows_weights(k, b), start=(k == 0), stop=(k == KT - 1))
        rows.then_inc(n.rows_done, 1)

    turn(0, 0)
    with pe.Fori(0, JT // 2 - 1) as pair:
        for par in range(2):
            j = pair * 2 + par
            turn(j + 1, 1 - par)
            rows_product(j, par)
    turn(JT - 1, 1)
    rows_product(JT - 2, 0)
    rows_product(JT - 1, 1)


def norm_on_scalar(act, n, rows_evacuation=None, beside=None):
    def copies(j, par):
        act.wait_ge(n.turned, j + 1 + FIRST)
        act.wait_ge(n.rows_done, j + 1)
        act.activation(n.full[:, par, :, :, :], n.turned_ps[:, par, :, :, :], ACT.Copy).then_inc(n.full_done, 1)
        act.activation(n.xhi[:, :, :, ds(j * P, P)], n.turned_ps[:, par, :, :, :], ACT.Copy).then_inc(n.hi_done, 1)
        if beside is not None:
            beside(j)

    def rows_out(j, par):
        if rows_evacuation is not None:
            act.wait_ge(n.rows_done, j + 1 + FIRST)
            rows_evacuation(act, j, par)

    copies(0, 0)
    with act.Fori(0, JT // 2 - 1) as pair:
        for par in range(2):
            j = pair * 2 + par
            copies(j + 1, 1 - par)
            rows_out(j, par)
    copies(JT - 1, 1)
    rows_out(JT - 2, 0)
    rows_out(JT - 1, 1)


class FfnBuffers:
    PARTS = ("gate", "up")

    def __init__(self, nc, scope, sem, name):
        def sb(n, shape, dt=F32R, scope=scope):
            return scope.enter_context(nc.sbuf_tensor(f"{name}_{n}", shape, dt))

        self.hi = {w: sb(f"{w}_hi", [P, KT, INTER]) for w in self.PARTS}
        self.lo = {w: sb(f"{w}_lo", [P, KT, INTER]) for w in self.PARTS}
        self.late_hi, self.late_lo = sb("late_hi", [P, JT, CHUNK]), sb("late_lo", [P, JT, CHUNK])
        self.routes = sb("routes", [P, JT, 2, 2, KEYS], F32)
        self.halves = [sb(f"x{part}", [P, KT, BATCH, SEQ]) for part in ("hi", "lo")]
        self.stage_scope = scope.enter_context(ExitStack())
        self.stage = {w: sb(f"{w}_stage", [P, KT, INTER], F32, self.stage_scope) for w in self.PARTS}
        self.late = sb("late_stage", [P, JT, CHUNK], F32, self.stage_scope)
        self.part_in = {w: sem(f"{name}_{w}_in") for w in self.PARTS}
        self.late_in = sem(f"{name}_late_in")

    def load(self, sp, dram):
        for w in self.PARTS:
            sp.dma_start(self.stage[w][:, :, :], dram[w].rearrange("(k p) f -> p k f", p=P)
                         ).then_inc(self.part_in[w], 16)
        sp.dma_start(self.late[:, 0:4, :].rearrange("p a (f d) -> p (a f) d", d=DIM),
                     dram["down"].rearrange("(f p) d -> p f d", p=P)).then_inc(self.late_in, 16)
        sp.dma_start(self.late[:, 4:6, :], dram["down_embed"].rearrange("(k p) f -> p k f", p=P)
                     ).then_inc(self.late_in, 16)
        sp.dma_start(self.late[:, 6:8, :].rearrange("p a (f d) -> p (a f) d", d=DIM),
                     dram["up_embed"].rearrange("(f p) d -> p f d", p=P)).then_inc(self.late_in, 16)


class RawProjections:

    def __init__(self, sem, space):
        flat = space[:, :, :, :].rearrange("p a j d -> p (a j d)")
        self.stage, self.lora_b, self.lora_a = {}, {}, {}
        for i, p in enumerate("qkv"):
            at = i * (KT + 2) * DIM
            self.stage[p] = flat[:, at:at + KT * DIM].rearrange("p (k o) -> p k o", k=KT)
            self.lora_b[p] = flat[0:RANK, at + KT * DIM:at + (KT + 1) * DIM]
            self.lora_a[p] = flat[0:RANK, at + (KT + 1) * DIM:at + (KT + 2) * DIM]
        self.weights_in = sem("proj_weights_in")

    def load(self, sp, dram):
        for p in "qkv":
            sp.dma_start(self.stage[p], dram[f"w{p}_t"].rearrange("(k p) o -> p k o", p=P)
                         ).then_inc(self.weights_in, 16)
            sp.dma_start(self.lora_b[p], dram[f"lora_b{p}"]).then_inc(self.weights_in, 16)
            sp.dma_start(self.lora_a[p], dram[f"lora_a{p}_t"]).then_inc(self.weights_in, 16)


def setup_block(nc, sem, dram, keep, buffers):
    with ExitStack() as scope:
        def sb(name, shape, dt):
            return scope.enter_context(nc.sbuf_tensor(name, shape, dt))

        wq_rows = sb("wq_rows", [RETRIEVAL // 2, 2, DIM], F32)
        keys_sb = sb("keys_sb", [RETRIEVAL // 2, 2, KEYS], F32)
        fold_ps = scope.enter_context(nc.psum_tensor("fold_ps", [P, KT, 2, 2, KEYS], F32))
        wq_in, keys_in = sem("wq_in"), sem("keys_in")
        x_in = [sem(f"x_in{c}") for c in range(CHUNKS)]
        ident_zero, folded, fold_out = sem("ident_zero"), sem("folded"), sem("fold_out")
        block = scope.enter_context(nc.Block())

        @block.sync
        def _(sp):
            sp.dma_start(wq_rows[:, :, :], dram["retrieval_t"].rearrange("(h d) x -> d h x", h=2)).then_inc(wq_in, 16)
            sp.dma_start(keys_sb[:, :, :], dram["keys"].rearrange("t d k -> d t k")).then_inc(keys_in, 16)
            x_tiles = dram["x"].rearrange("(t p) d -> p t d", p=P)
            for c in range(CHUNKS):
                sp.dma_start(keep["x"][:, c * CT:(c + 1) * CT, :], x_tiles[:, c * CT:(c + 1) * CT, :]
                             ).then_inc(x_in[c], 16)
            buffers.load(sp, dram)

        @block.gpsimd
        def _(pool):
            pool.memset(keep["ident"][:, :], 0.0).then_inc(ident_zero, 1)
            pool.memset(keep["minus_half"][:, :], -0.5).then_inc(keep["ident_done"], 1)
            pool.wait_ge(ident_zero, 1)
            pool.affine_select(out=keep["ident"][:, :], in_=keep["ident"][:, :], compare_op=ALU.not_equal,
                               fill=1.0, base=0, pattern=[[-1, P]], channel_multiplier=1
                               ).then_inc(keep["ident_done"], 1)

        @block.tensor
        def _(pe):
            pe.wait_ge(wq_in, 16)
            pe.wait_ge(keys_in, 16)
            for half in range(2):
                for k in range(KT):
                    for t in range(2):
                        fold = pe.matmul(fold_ps[:, k, t, half, :], wq_rows[:, half, k * P:(k + 1) * P],
                                         keys_sb[:, t, :], start=True, stop=True)
            fold.then_inc(folded, 1)

        @block.scalar
        def _(act):
            act.wait_ge(folded, 1)
            act.activation(keep["route_w"][:, :, :, :, :].rearrange("p k t h y -> p (k t h y)"),
                           fold_ps[:, :, :, :, :].rearrange("p k t h y -> p (k t h y)"), ACT.Copy
                           ).then_inc(fold_out, 1)

        @block.vector
        def _(v):
            for c in range(CHUNKS):
                v.wait_ge(x_in[c], 16)
                for t in range(c * CT, (c + 1) * CT):
                    v.bn_stats(keep["stats"][:, t, :], keep["x"][:, t, :]).then_inc(keep["stats_done"], 1)


def ffn_block(nc, sem_of, dram, keep, buffers, layer, raw=None):
    store = layer == 1
    x_sb, ident = keep["x"], keep["ident"]
    name = f"ffn{layer}"
    with ExitStack() as scope:
        def sb(n, shape, dt):
            return scope.enter_context(nc.sbuf_tensor(f"{name}_{n}", shape, dt))

        def psum(n, shape, dt):
            return scope.enter_context(nc.psum_tensor(f"{name}_{n}", shape, dt))

        def sem(n):
            return sem_of(f"{name}_{n}")

        parts, hi, lo, late_hi, late_lo = buffers.PARTS, buffers.hi, buffers.lo, buffers.late_hi, buffers.late_lo
        stage, late, routes, halves = buffers.stage, buffers.late, buffers.routes, buffers.halves

        part_hi, part_lo = sem("part_hi"), sem("part_lo")
        late_hi_done, late_lo_done = sem("late_hi_done"), sem("late_lo_done")
        late_even_done = sem("late_even_done")
        route_in = sem("route_in")
        scored = sem("scored")
        route_exp = sem("route_exp")
        scaled = sem("scaled")
        grid_done = sem("grid_done")
        mixed = sem("mixed")
        gate_ready, up_ready = sem("gate_ready"), sem("up_ready")
        tanh_done, gated_done = sem("tanh_done"), sem("gated_done")
        hidden_done = sem("hidden_done")
        hidden_hi_done = sem("hidden_hi_done")
        hidden_lo_done = sem("hidden_lo_done")
        down_done = sem("down_done")
        mix_turned = sem("mix_turned")
        out_copied = sem("out_copied")
        out_turned = sem("out_turned")
        x_updated = sem("x_updated")
        stored = sem("stored")

        with ExitStack() as norm_scope:
            def norm_sb(n, shape, dt):
                return norm_scope.enter_context(nc.sbuf_tensor(n, shape, dt))

            def norm_psum(n, shape, dt):
                return norm_scope.enter_context(nc.psum_tensor(n, shape, dt))

            n = Norm(f"{name}_norm", norm_sb, norm_psum, sem_of, halves, KEYS * 2)
            block = norm_scope.enter_context(nc.Block())

            @block.gpsimd
            def _(pool):
                norm_on_gpsimd(pool, n, keep["minus_half"][:, :])
                for i, w in enumerate(parts):
                    pool.wait_ge(part_hi, i + 1)
                    pool.tensor_tensor(lo[w][:, :, :], stage[w][:, :, :], hi[w][:, :, :].bitcast(F32),
                                       ALU.subtract).then_inc(part_lo, 1)
                with pool.Fori(0, JT // 2) as pair:
                    j = pair * 2 + 1
                    pool.wait_ge(late_hi_done, j + 1)
                    pool.tensor_tensor(late_lo[:, j, :], late[:, j, :], late_hi[:, j, :].bitcast(F32),
                                       ALU.subtract).then_inc(late_lo_done, 1)

            @block.tensor
            def _(pe):
                pe.wait_ge(keep["ident_done"], 2)
                norm_on_tensor(pe, n, ident[:, :],
                               lambda k, b: keep["route_w"][:, k, b, :, :].rearrange("p h k -> p (h k)"))

            @block.scalar
            def _(act):
                act.sem_inc(n.rows_out, FIRST)

                def routes_out(act, j, par):
                    act.activation(routes[:, j, :, :, :],
                                   n.rows_ps[:, par, 0:4 * KEYS].rearrange("p (b h k) -> p b h k", b=2, h=2),
                                   ACT.Copy).then_inc(n.rows_out, 1)

                def round_late(j):
                    if isinstance(j, int) and j == 0:
                        act.wait_ge(buffers.late_in, 48)
                    act.activation(late_hi[:, j, :], late[:, j, :], ACT.Copy).then_inc(late_hi_done, 1)

                for w in parts:
                    act.wait_ge(buffers.part_in[w], 16)
                    act.activation(hi[w][:, :, :], stage[w][:, :, :], ACT.Copy).then_inc(part_hi, 1)
                norm_on_scalar(act, n, routes_out, round_late)

            @block.vector
            def _(v):
                v.sem_inc(n.lo_done, FIRST)

                def split_late(j):
                    v.wait_ge(late_hi_done, j + 1)
                    v.tensor_tensor(late_lo[:, j, :], late[:, j, :], late_hi[:, j, :].bitcast(F32),
                                    ALU.subtract).then_inc(late_even_done, 1)

                variances_on_vector(v, n, keep["stats"])
                norm_on_vector(v, n, x_sb, beside=split_late)

        buffers.stage_scope.close()

        DOWN_LAG, AHEAD, HIDDEN_RING, SPLIT_RING = 2, 3, 3, 4
        hidden = sb("hidden", [P, HIDDEN_RING, CHUNK], F32)
        hidden_hi = sb("hidden_hi", [P, SPLIT_RING, CHUNK], F32R)
        hidden_lo = sb("hidden_lo", [P, SPLIT_RING, CHUNK], F32R)
        out_rows = sb("out_rows", [P, KT, CHUNK], F32)
        tanh = sb("tanh", [P, 2, CHUNK], F32)
        gated = sb("gated", [P, 2, CHUNK], F32)
        mix = sb("mix", [P, 2, 2, EXPERTS], F32)
        r = sb("r", [P, 2, 2, 2, KEYS], F32)
        best = sb("best", [P, 2, 2, 2, TOP], F32)
        below = sb("below", [P, 2, 2, 2, KEYS], F32)
        expo = sb("expo", [P, 2, 2, 2, KEYS], F32)
        pairs = sb("pairs", [P, 2, 2, TOP, TOP], F32)
        top = sb("top", [P, 2, 2, TOP], F32)
        top_below = sb("top_below", [P, 2, 2, TOP], F32)
        top_exp = sb("top_exp", [P, 2, 2, TOP], F32)
        total = sb("total", [P, 2, 2], F32)
        inverse = sb("inverse", [P, 2, 2], F32)
        row_exp = sb("row_exp", [P, 2, 2, GRID_ROWS], F32)
        sums = sb("sums", [P, 2, 2, GRID_ROWS, KEYS], F32)
        grid = sb("grid", [P, 2, 2, GRID_ROWS, KEYS], F32)
        inside = sb("inside", [P, 2, 2], F32)
        clipped = sb("clipped", [P, 2, 2], F32)

        gate_ps = psum("gate_ps", [P, 2, CHUNK], F32)
        up_ps = psum("up_ps", [P, 2, CHUNK], F32)
        mix_ps = psum("mix_ps", [P, 2, CHUNK], F32)
        out_ps = psum("out_ps", [P, KT, CHUNK], F32)
        block = scope.enter_context(nc.Block())
        SCORE_STEPS, SCALE_STEPS, MIX_STEPS = 11, 3, 4
        EXPS_AFTER = (2, 4)

        def gate_weight(u):
            if u < FT:
                at = slice(u * P, (u + 1) * P)
                return [(hi["gate"][:, k, at], lo["gate"][:, k, at]) for k in range(KT)]
            at = slice((u - FT) * P, (u - FT + 1) * P)
            return [(late_hi[:, 4 + k, at], late_lo[:, 4 + k, at]) for k in range(KT)]

        def up_weight(u):
            at = slice(u * P, (u + 1) * P)
            return [(hi["up"][:, k, at], lo["up"][:, k, at]) for k in range(KT)]

        def down_weight(u, k):
            piece, column = (u if u < FT else u - FT + 12) // 2, u % 2 * DIM + k * P
            return late_hi[:, piece, column:column + P], late_lo[:, piece, column:column + P]

        @block.tensor
        def _(pe):
            def unit(c, u):
                tokens = n.token_halves(c)
                if u < FT:
                    pe.wait_ge(hidden_done, c * UNITS + u + 1)
                    product3(pe, gate_ps[:, u % 2, :], gate_weight(u), tokens).then_inc(gate_ready, 1)
                    product3(pe, up_ps[:, u % 2, :], up_weight(u), tokens).then_inc(up_ready, 1)
                    return
                e = u - FT
                pe.wait_ge(gated_done, c * UNITS + u - 1)
                product3(pe, gate_ps[:, u % 2, :], gate_weight(u), tokens).then_inc(gate_ready, 1)
                if e == 0:
                    pe.wait_ge(mixed, (c + 1) * 2 * MIX_STEPS)
                    pe.wait_ge(x_updated, c * CT + 1)
                if e >= 2:
                    pe.wait_ge(hidden_done, c * UNITS + u + 1)
                for jh in range(4):
                    turn = pe.transpose(mix_ps[:, e % 2, jh * P:(jh + 1) * P],
                                        mix[:, jh // 2, jh % 2, e * P:(e + 1) * P], ident[:, :])
                turn.then_inc(mix_turned, 1)

            def down(c, u):
                pe.wait_ge(hidden_lo_done, c * UNITS + u + 1 + HIDDEN_RING)
                for k in range(KT):
                    w_hi, w_lo = down_weight(u, k)
                    x_hi, x_lo = hidden_hi[:, u % SPLIT_RING, :], hidden_lo[:, u % SPLIT_RING, :]
                    pe.matmul(out_ps[:, k, :], w_hi, x_hi, start=(u == 0), stop=False)
                    pe.matmul(out_ps[:, k, :], w_lo, x_hi, start=False, stop=False)
                    out = pe.matmul(out_ps[:, k, :], w_hi, x_lo, start=False, stop=(u == UNITS - 1))
                out.then_inc(down_done, 1)

            def turn_out(c):
                pe.wait_ge(out_copied, (c + 1) * KT)
                for tt in range(CT):
                    for k in range(KT):
                        at = tt % 2 * DIM + k * P
                        turn = pe.transpose(mix_ps[:, tt // 2, at:at + P], out_rows[:, k, tt * P:(tt + 1) * P],
                                            ident[:, :])
                turn.then_inc(out_turned, 1)

            pe.sem_inc(down_done, SPLIT_RING)
            pe.wait_ge(part_lo, len(parts))
            pe.wait_ge(late_lo_done, JT // 2)
            pe.wait_ge(late_even_done, JT // 2)
            for u in range(AHEAD):
                unit(0, u)
            with pe.Fori(0, CHUNKS - 1) as c:
                down(c, 0)
                for u in range(AHEAD, UNITS):
                    unit(c, u)
                    down(c, u - DOWN_LAG)
                for u in range(DOWN_LAG):
                    unit(c + 1, u)
                    down(c, UNITS - DOWN_LAG + u)
                unit(c + 1, DOWN_LAG)
                turn_out(c)
            down(CHUNKS - 1, 0)
            for u in range(AHEAD, UNITS):
                unit(CHUNKS - 1, u)
                down(CHUNKS - 1, u - DOWN_LAG)
            for u in range(UNITS - DOWN_LAG, UNITS):
                down(CHUNKS - 1, u)
            turn_out(CHUNKS - 1)

        @block.scalar
        def _(act):
            def fetch_routes(j, jp):
                act.activation(r[:, jp, :, :, :], routes[:, j, :, :, :], ACT.Copy).then_inc(route_in, 1)

            def route_exps(j, jp):
                act.wait_ge(scored, (j + 1) * SCORE_STEPS)
                act.activation(expo[:, jp, :, :, :], below[:, jp, :, :, :], ACT.Exp).then_inc(route_exp, 1)
                act.activation(top_exp[:, jp, :, :], top_below[:, jp, :, :], ACT.Exp).then_inc(route_exp, 1)

            def unit(c, u):
                if u == 0:
                    for jp in range(2):
                        fetch_routes(c * 2 + jp, jp)
                act.wait_ge(gate_ready, c * UNITS + u + 1)
                if u >= 2:
                    act.wait_ge(gated_done, c * UNITS + u - 1)
                act.activation(tanh[:, u % 2, :], gate_ps[:, u % 2, :], ACT.Tanh, scale=0.5).then_inc(tanh_done, 1)
                if u in EXPS_AFTER:
                    jp = EXPS_AFTER.index(u)
                    route_exps(c * 2 + jp, jp)

            def round_hidden(c, u):
                act.wait_ge(hidden_done, c * UNITS + u + 1 + FIRST)
                act.wait_ge(down_done, c * UNITS + u + 1)
                act.activation(hidden_hi[:, u % SPLIT_RING, :], hidden[:, u % HIDDEN_RING, :], ACT.Copy
                               ).then_inc(hidden_hi_done, 1)

            def copy_out(c):
                act.wait_ge(down_done, (c + 1) * UNITS + SPLIT_RING)
                for k in range(KT):
                    act.activation(out_rows[:, k, :], out_ps[:, k, :], ACT.Copy).then_inc(out_copied, 1)

            unit(0, 0)
            for u in range(1, AHEAD):
                unit(0, u)
                round_hidden(0, u - 1)
            with act.Fori(0, CHUNKS - 1) as c:
                for u in range(AHEAD, UNITS):
                    unit(c, u)
                    round_hidden(c, u - 1)
                unit(c + 1, 0)
                round_hidden(c, UNITS - 1)
                unit(c + 1, 1)
                round_hidden(c + 1, 0)
                copy_out(c)
                unit(c + 1, 2)
                round_hidden(c + 1, 1)
            for u in range(AHEAD, UNITS):
                unit(CHUNKS - 1, u)
                round_hidden(CHUNKS - 1, u - 1)
            round_hidden(CHUNKS - 1, UNITS - 1)
            copy_out(CHUNKS - 1)

        @block.gpsimd
        def _(pool):
            def expert_grid(j, jp):
                pool.wait_ge(scaled, (j + 1) * SCALE_STEPS)
                for h in range(2):
                    row = row_exp[:, jp, h, :].unsqueeze(2).broadcast_to([P, GRID_ROWS, KEYS])
                    col = expo[:, jp, 1, h, :].unsqueeze(1).broadcast_to([P, GRID_ROWS, KEYS])
                    pool.tensor_tensor(grid[:, jp, h, :, :], row, col, ALU.mult).then_inc(grid_done, 1)

            pool.sem_inc(hidden_lo_done, HIDDEN_RING)
            with pool.Fori(0, CHUNKS) as c:
                for u in range(UNITS):
                    pool.wait_ge(hidden_hi_done, c * UNITS + u + 1)
                    pool.tensor_tensor(hidden_lo[:, u % SPLIT_RING, :], hidden[:, u % HIDDEN_RING, :],
                                       hidden_hi[:, u % SPLIT_RING, :].bitcast(F32), ALU.subtract
                                       ).then_inc(hidden_lo_done, 1)
                    if u in (4, 5):
                        expert_grid(c * 2 + u - 4, u - 4)

        @block.vector
        def _(v):
            def pair_sums(jp, h):
                v.tensor_tensor(sums[:, jp, h, :, :],
                                r[:, jp, 0, h, 0:GRID_ROWS].unsqueeze(2).broadcast_to([P, GRID_ROWS, KEYS]),
                                r[:, jp, 1, h, :].unsqueeze(1).broadcast_to([P, GRID_ROWS, KEYS]),
                                ALU.add).then_inc(scored, 1)

            def score_keys(j, jp):
                v.wait_ge(route_in, j + 1)
                pair_sums(jp, 0)
                for b in range(2):
                    for h in range(2):
                        v.max(best[:, jp, b, h, :], r[:, jp, b, h, :]).then_inc(scored, 1)
                v.wait_ge(scored, j * SCORE_STEPS + 5)
                v.tensor_tensor(pairs[:, jp, :, :, :],
                                best[:, jp, 0, :, :].unsqueeze(3).broadcast_to([P, 2, TOP, TOP]),
                                best[:, jp, 1, :, :].unsqueeze(2).broadcast_to([P, 2, TOP, TOP]),
                                ALU.add).then_inc(scored, 1)
                v.tensor_tensor(below[:, jp, :, :, :].rearrange("p b h k -> p (b h) k"),
                                r[:, jp, :, :, :].rearrange("p b h k -> p (b h) k"),
                                best[:, jp, :, :, 0:1].rearrange("p b h o -> p (b h) o").broadcast_to([P, 4, KEYS]),
                                ALU.subtract).then_inc(scored, 1)

            def score_pairs(j, jp):
                v.wait_ge(scored, j * SCORE_STEPS + 6)
                pair_sums(jp, 1)
                for h in range(2):
                    v.max(top[:, jp, h, :], pairs[:, jp, h, :, :]).then_inc(scored, 1)
                v.wait_ge(scored, j * SCORE_STEPS + 10)
                v.tensor_tensor(top_below[:, jp, :, :], top[:, jp, :, :],
                                top[:, jp, :, 0:1].broadcast_to([P, 2, TOP]), ALU.subtract).then_inc(scored, 1)

            def scale(j, jp):
                v.wait_ge(route_exp, (j + 1) * 2)
                v.reduce_sum(total[:, jp, :], top_exp[:, jp, :, :], axis=AXIS_X).then_inc(scaled, 1)
                v.wait_ge(scaled, j * SCALE_STEPS + 1)
                v.reciprocal(inverse[:, jp, :], total[:, jp, :]).then_inc(scaled, 1)
                v.wait_ge(scaled, j * SCALE_STEPS + 2)
                v.tensor_tensor(row_exp[:, jp, :, :], expo[:, jp, 0, :, 0:GRID_ROWS],
                                inverse[:, jp, :].unsqueeze(2).broadcast_to([P, 2, GRID_ROWS]),
                                ALU.mult).then_inc(scaled, 1)

            def blend(j, jp):
                v.wait_ge(grid_done, (j + 1) * 2)
                v.wait_ge(scored, (j + 1) * SCORE_STEPS)
                for h in range(2):
                    v.scalar_tensor_tensor(out=mix[:, jp, h, :],
                                           in0=sums[:, jp, h, :, :].rearrange("p a b -> p (a b)"),
                                           scalar=top[:, jp, h, TOP - 1:TOP],
                                           in1=grid[:, jp, h, :, :].rearrange("p a b -> p (a b)"),
                                           op0=ALU.is_ge, op1=ALU.mult,
                                           accum_out=inside[:, jp, h:h + 1]).then_inc(mixed, 1)
                v.wait_ge(mixed, j * MIX_STEPS + 2)
                v.tensor_scalar(clipped[:, jp, :], inside[:, jp, :], -1.0, 1.0, ALU.mult, ALU.add).then_inc(mixed, 1)
                v.wait_ge(mixed, j * MIX_STEPS + 3)
                v.tensor_tensor(mix[:, jp, :, EXPERTS - 1], mix[:, jp, :, EXPERTS - 1], clipped[:, jp, :],
                                ALU.add).then_inc(mixed, 1)

            def gate_unit(c, u):
                v.wait_ge(tanh_done, c * UNITS + u + 1)
                v.scalar_tensor_tensor(out=gated[:, u % 2, :], in0=tanh[:, u % 2, :], scalar=1.0,
                                       in1=gate_ps[:, u % 2, :], op0=ALU.add, op1=ALU.mult).then_inc(gated_done, 1)
                v.wait_ge(gated_done, c * UNITS + u + 1)

            def unit(c, u):
                gate_unit(c, u)
                v.wait_ge(hidden_lo_done, c * UNITS + u + 1)
                if u < FT:
                    v.wait_ge(up_ready, c * FT + u + 1)
                    v.tensor_tensor(hidden[:, u % HIDDEN_RING, :], gated[:, u % 2, :], up_ps[:, u % 2, :],
                                    ALU.mult).then_inc(hidden_done, 1)
                    if u < 4:
                        jp = u // 2
                        if u % 2 == 0:
                            score_keys(c * 2 + jp, jp)
                        else:
                            score_pairs(c * 2 + jp, jp)
                    elif u < 6:
                        scale(c * 2 + u - 4, u - 4)
                    else:
                        blend(c * 2 + u - 6, u - 6)
                    return
                e = u - FT
                v.wait_ge(mix_turned, c * ET + e + 1)
                v.tensor_tensor(hidden[:, u % HIDDEN_RING, :].rearrange("p (j i h) -> p j i h", j=2, h=2),
                                gated[:, u % 2, :].rearrange("p (j i h) -> p j i h", j=2, h=2),
                                mix_ps[:, e % 2, :].rearrange("p (j h i) -> p j i h", j=2, h=2),
                                ALU.mult).then_inc(hidden_done, 1)

            def update(c):
                v.wait_ge(out_turned, c + 1)
                for tt in range(CT):
                    v.scalar_tensor_tensor(out=x_sb[:, c * CT + tt, :],
                                           in0=mix_ps[:, tt // 2, tt % 2 * DIM:(tt % 2 + 1) * DIM], scalar=0.25,
                                           in1=x_sb[:, c * CT + tt, :], op0=ALU.mult, op1=ALU.add
                                           ).then_inc(x_updated, 1)
                if not store:
                    for tt in range(CT):
                        v.wait_ge(x_updated, c * CT + tt + 2)
                        v.bn_stats(keep["stats"][:, c * CT + tt, :], x_sb[:, c * CT + tt, :]
                                   ).then_inc(keep["stats_done"], 1)

            v.sem_inc(hidden_done, FIRST)
            v.sem_inc(x_updated, 1)
            for u in range(AHEAD):
                unit(0, u)
            with v.Fori(0, CHUNKS - 1) as c:
                for u in range(AHEAD, UNITS):
                    unit(c, u)
                for u in range(AHEAD):
                    unit(c + 1, u)
                update(c)
            for u in range(AHEAD, UNITS):
                unit(CHUNKS - 1, u)
            update(CHUNKS - 1)

        @block.sync
        def _(sp):
            if raw is not None:
                raw.load(sp, dram)
            if store:
                out_tiles = dram["out"].rearrange("(t p) d -> p t d", p=P)
                with sp.Fori(0, CHUNKS) as c:
                    sp.wait_ge(x_updated, (c + 1) * CT + 1)
                    sp.dma_start(out_tiles[:, ds(c * CT, CT), :], x_sb[:, ds(c * CT, CT), :]).then_inc(stored, 16)
                sp.wait_ge(stored, CHUNKS * 16)


SLOTS = 4
STACK_ROWS = 4 * HD
STACK_DMAS = 17


class Stacks:

    def __init__(self, nc, scope, sem, s):
        self.q = scope.enter_context(nc.sbuf_tensor(f"q_stack{s}", [P, 2, SEQ], F32R))
        self.k = scope.enter_context(nc.sbuf_tensor(f"k_stack{s}", [P, 2, SEQ], F32R))
        self.loaded = sem(f"stacks_in{s}")

    def load(self, sp, attn, s, it, cleared=None):
        for stack, parts in ((self.q, ("q_hi", "q_hi", "q_lo", "q_lo")), (self.k, ("k_hi", "k_lo", "k_hi", "k_lo"))):
            for i, part in enumerate(parts):
                source = attn[part][:, :, :].rearrange("p f n -> p (f n)")
                for j in range(2):
                    at = s * 2 * HD + j * HD
                    sp.dma_start(stack[i * HD:(i + 1) * HD, j, :].bitcast(F32),
                                 source[at:at + HD, ds(it * SEQ, SEQ)].bitcast(F32)).then_inc(self.loaded, 16)
        if cleared is not None:
            sp.wait_ge(*cleared)
        sp.dma_start(self.q[STACK_ROWS:STACK_ROWS + 1, :, :].bitcast(F32),
                     self.q[STACK_ROWS + 1:STACK_ROWS + 2, :, :].bitcast(F32)).then_inc(self.loaded, 16)


def project_block(nc, sem, dram, keep, attn, raw):
    x_sb, ident = keep["x"], keep["ident"]
    with ExitStack() as scope:
        def sb(n, shape, dt):
            return scope.enter_context(nc.sbuf_tensor(f"proj_{n}", shape, dt))

        def psum(n, shape, dt):
            return scope.enter_context(nc.psum_tensor(f"proj_{n}", shape, dt))

        wide = ("q", "k")
        QK = len(wide) * KT
        w_hi = {p: sb(f"w{p}_hi", [P, KT, DIM], F32R) for p in wide}
        w_lo = {p: sb(f"w{p}_lo", [P, KT, DIM], F32R) for p in wide}
        w_v = sb("wv", [P, KT, DIM], F32)
        bias_v = sb("bias_v", [P, DIM], F32)
        bias = {p: sb(f"bias_{p}", [P, KT], F32) for p in wide}
        halves = [sb(f"x{part}", [P, KT, BATCH, SEQ], F32R) for part in ("hi", "lo")]
        n = Norm("proj_norm", sb, psum, sem, halves, DIM)
        stage, lora_b, lora_a, weights_in = raw.stage, raw.lora_b, raw.lora_a, raw.weights_in
        whole = {p: sb(f"w{p}_whole", [P, KT, DIM], F32) for p in wide} | {"v": w_v}
        qk_ps = psum("qk_ps", [P, 2 * KT, CHUNK], F32)

        bias_in = sem("proj_bias_in")
        first_set = sem("first_set")
        stacks0 = attn["stacks0"]
        update_ready = sem("proj_update_ready")
        whole_done = sem("proj_whole_done")
        w_hi_done, w_lo_done = sem("proj_w_hi_done"), sem("proj_w_lo_done")
        qk_ready = sem("proj_qk_ready")
        qk_hi_done = sem("proj_qk_hi_done")
        qk_lo_done = sem("proj_qk_lo_done")
        block = scope.enter_context(nc.Block())

        @block.sync
        def _(sp):
            for p in wide:
                sp.dma_start(bias[p][:, :], dram[f"b{p}_columns"]).then_inc(bias_in, 16)
            sp.dma_start(bias_v[:, :], dram["bv"].partition_broadcast(P)).then_inc(bias_in, 16)
            sp.wait_ge(qk_lo_done, QK + CHUNKS // BATCH * QK)
            stacks0.load(sp, attn, 0, 0, (first_set, 3))
            sp.wait_ge(stacks0.loaded, STACK_DMAS * 16)

        @block.gpsimd
        def _(pool):
            norm_on_gpsimd(pool, n, keep["minus_half"][:, :])
            pool.wait_ge(n.rstd_done, JT // 2)
            for i, p in enumerate(wide):
                pool.wait_ge(w_hi_done, i + 1)
                pool.tensor_tensor(w_lo[p][:, :, :], whole[p][:, :, :], w_hi[p][:, :, :].bitcast(F32),
                                   ALU.subtract).then_inc(w_lo_done, 1)
            pool.wait_ge(w_lo_done, len(wide))
            pool.memset(stacks0.q[STACK_ROWS:P, :, :].bitcast(F32), 0.0).then_inc(first_set, 1)
            pool.wait_ge(first_set, 1)
            pool.memset(stacks0.k[STACK_ROWS:P, :, :].bitcast(F32), 0.0).then_inc(first_set, 1)
            pool.wait_ge(first_set, 2)
            pool.memset(stacks0.k[STACK_ROWS:STACK_ROWS + 1, :, :].bitcast(F32), 1.0).then_inc(first_set, 1)

        @block.tensor
        def _(pe):
            pe.wait_ge(weights_in, 3 * 48)
            for i, p in enumerate("qkv"):
                for k in range(KT):
                    update = pe.matmul(qk_ps[:, i, k * DIM:(k + 1) * DIM], lora_b[p][:, k * P:(k + 1) * P], lora_a[p],
                                       start=True, stop=True)
                update.then_inc(update_ready, 1)
            pe.wait_ge(whole_done, 3)
            norm_on_tensor(pe, n, ident[:, :], lambda k, b: w_v[:, k, :])
            pe.wait_ge(w_lo_done, len(wide))
            with pe.Fori(0, CHUNKS) as c:
                tokens = n.token_halves(c)
                for i, p in enumerate(wide):
                    for f in range(KT):
                        at = slice(f * P, (f + 1) * P)
                        pe.wait_ge(qk_lo_done, c * QK + i * KT + f + 1)
                        product3(pe, qk_ps[:, i * KT + f, :],
                                 [(w_hi[p][:, k, at], w_lo[p][:, k, at]) for k in range(KT)],
                                 tokens).then_inc(qk_ready, 1)

        @block.scalar
        def _(act):
            act.wait_ge(whole_done, len(wide))
            for i, p in enumerate(wide):
                act.activation(w_hi[p][:, :, :], whole[p][:, :, :], ACT.Copy).then_inc(w_hi_done, 1)
            norm_on_scalar(act, n)
            act.wait_ge(bias_in, 48)
            with act.Fori(0, CHUNKS) as c:
                for i, p in enumerate(wide):
                    for f in range(KT):
                        act.wait_ge(qk_ready, c * QK + i * KT + f + 1)
                        act.activation(attn[f"{p}_hi"][:, f, ds(c * CHUNK, CHUNK)], qk_ps[:, i * KT + f, :],
                                       ACT.Identity, bias=bias[p][:, f:f + 1]).then_inc(qk_hi_done, 1)

        @block.vector
        def _(v):
            v.sem_inc(n.lo_done, FIRST)
            v.sem_inc(n.rows_out, FIRST)
            v.sem_inc(qk_lo_done, QK)
            variances_on_vector(v, n, keep["stats"])
            for i, p in enumerate("qkv"):
                v.wait_ge(update_ready, i + 1)
                update = qk_ps[:, i, :].rearrange("p (k o) -> p k o", k=KT)
                v.scalar_tensor_tensor(out=whole[p][:, :, :], in0=update, scalar=LORA_SCALE,
                                       in1=stage[p], op0=ALU.mult, op1=ALU.add).then_inc(whole_done, 1)
            v.wait_ge(bias_in, 48)

            def v_rows_out(v, j, par):
                for b in range(BATCH):
                    out = attn["v"][:, :, b, j, :, :]
                    done = v.tensor_tensor(
                        out, n.rows_ps[:, par, b * DIM:(b + 1) * DIM].rearrange("p (f h d) -> p f h d", f=KT, d=HD),
                        bias_v[:, :].rearrange("p (f h d) -> p f h d", f=KT, d=HD), ALU.add)
                done.then_inc(n.rows_out, 1)

            norm_on_vector(v, n, x_sb, v_rows_out)
            with v.Fori(0, CHUNKS) as c:
                for i, p in enumerate(wide):
                    for f in range(KT):
                        v.wait_ge(qk_hi_done, c * QK + i * KT + f + 1)
                        at = ds(c * CHUNK, CHUNK)
                        v.scalar_tensor_tensor(out=attn[f"{p}_lo"][:, f, at], in0=qk_ps[:, i * KT + f, :],
                                               scalar=bias[p][:, f:f + 1], in1=attn[f"{p}_hi"][:, f, at].bitcast(F32),
                                               op0=ALU.add, op1=ALU.subtract).then_inc(qk_lo_done, 1)


def attention_block(nc, sem, dram, keep, attn):
    HALF = SEQ // 2
    ITS = KT * BATCH
    KEY_TILES = SEQ // P
    STRIP = 32
    ROWS = STACK_ROWS
    MAXES = 2 * KEY_TILES * 2
    SCORES = KEY_TILES * 2 * 2
    EARLY = 12
    TURN_AT = 6
    RING = 3
    assert MAXES % RING == SCORES % RING == 2
    last_reader = lambda i: (i if i >= RING else (1, 2, 0)[i]) + 1
    with ExitStack() as scope:
        def sb(n, shape, dt):
            return scope.enter_context(nc.sbuf_tensor(n, shape, dt))

        def psum(n, shape, dt):
            return scope.enter_context(nc.psum_tensor(n, shape, dt))

        stacks = [attn["stacks0"]] + [Stacks(nc, scope, sem, s) for s in range(1, SLOTS)]
        q_stack, k_stack = [stack.q for stack in stacks], [stack.k for stack in stacks]
        values = [sb(f"values{s}", [P, KEY_TILES, 2, STRIP], F32) for s in range(SLOTS)]
        probs = sb("probs", [P, 2, 2, SEQ], F32)
        maxima = sb("maxima", [P, 2, MAXES // 2, 2], F32)
        maximum = sb("maximum", [P, 2, MAXES // 2], F32)
        max_rows = sb("max_rows", [MAXES // 2, 2, P], F32R)
        mixed = sb("mixed_t", [P, HALF], F32)
        inverse = sb("inverse_sum", [P, KEY_TILES // 2, 4], F32)
        bias_o = sb("bias_o", [P, DIM], F32)
        score_ps = psum("score_ps", [P, RING, HALF], F32)
        max_ps = psum("max_ps", [P, RING, HALF], F32)
        mixed_ps = psum("mixed_ps", [P, HALF], F32)
        turn_ps = psum("turn_ps", [P, KEY_TILES // 2, 4, STRIP], F32)

        stacks_in = [stack.loaded for stack in stacks]
        max_in = [sem(f"max_in{s}") for s in range(SLOTS)]
        q_cleared = sem("q_cleared")
        ones_set = sem("ones_set")
        v_set = sem("v_set")
        values_in = sem("values_in")
        early_scored = sem("early_scored")
        early_max = sem("early_max")
        tile_scored = sem("tile_scored")
        tile_max = sem("tile_max")
        group_max = sem("group_max")
        max_turned = sem("max_turned")
        max_negated = sem("max_negated")
        scores_ready = sem("scores_ready")
        probs_ready = sem("probs_ready")
        probs_used = sem("probs_used")
        mixed_out = sem("mixed_out")
        mixed_turned = [sem(f"mixed_turned{s}") for s in range(SLOTS)]
        inverted = sem("inverted")
        bias_in, x_biased = sem("o_bias_in"), sem("x_biased")
        group_out = sem("group_out")
        block = scope.enter_context(nc.Block())

        @block.sync
        def _(sp):
            def load_maxima(count, par, s):
                sp.wait_ge(max_negated, count)
                sp.dma_start(q_stack[s][ROWS:ROWS + 1, :, :].rearrange("o j (t q) -> o (j t) q", q=P).bitcast(F32),
                             max_rows[:, par, :].bitcast(F32)).then_inc(max_in[s], 16)

            sp.dma_start(bias_o[:, :], dram["bo"].partition_broadcast(P)).then_inc(bias_in, 16)
            for s in range(1, SLOTS):
                if s == SLOTS - 1:
                    load_maxima(1, 0, 0)
                stacks[s].load(sp, attn, s, 0, (q_cleared, s))
            with sp.Fori(0, ITS - 1) as it:
                for s in range(SLOTS):
                    load_maxima(it * SLOTS + s + 2, (s + 1) % 2, (s + 1) % SLOTS)
                    sp.wait_ge(mixed_turned[s], it + 2)
                    stacks[s].load(sp, attn, s, it + 1)
            for s in range(SLOTS - 1):
                load_maxima((ITS - 1) * SLOTS + s + 2, (s + 1) % 2, s + 1)

        @block.gpsimd
        def _(pool):
            for s in range(SLOTS):
                pool.memset(values[s][:, :, :, :], 0.0).then_inc(v_set, 1)
                pool.wait_ge(v_set, 2 * s + 1)
                pool.memset(values[s][:, :, :, HD:HD + 1], 1.0).then_inc(v_set, 1)
                pool.wait_ge(v_set, 2 * s + 2)
                if s >= 1:
                    pool.memset(k_stack[s][ROWS:P, :, :].bitcast(F32), 0.0).then_inc(ones_set, 1)
                    pool.wait_ge(ones_set, 2 * s - 1)
                    pool.memset(k_stack[s][ROWS:ROWS + 1, :, :].bitcast(F32), 1.0).then_inc(ones_set, 1)
                    pool.wait_ge(ones_set, 2 * s)
            by_group = attn["v"][:, :, :, :, :, :].rearrange("p f b j h d -> p (f b) j (h d)")
            with pool.Fori(0, ITS) as it:
                for s in range(SLOTS):
                    pool.wait_ge(mixed_turned[s], it + 1)
                    pool.tensor_copy(values[s][:, :, :, 0:HD],
                                     by_group[:, it, :, s * 2 * HD:(s + 1) * 2 * HD]
                                     .rearrange("p j (h d) -> p j h d", d=HD)).then_inc(values_in, 1)

        @block.tensor
        def _(pe):
            ident = attn["ident"]

            def max_scores(group, s, i, scored, taken):
                j, qt, half = i // 16, i // 2 % KEY_TILES, i % 2
                pe.wait_ge(taken, group * MAXES + last_reader(i))
                pe.matmul(max_ps[:, i % RING, :], q_stack[s][:, j, qt * P:(qt + 1) * P],
                          k_stack[s][:, j, half * HALF:(half + 1) * HALF], start=True, stop=True
                          ).then_inc(scored, 1)

            def turn_group_max(count, par, groups_out):
                pe.wait_ge(group_max, count)
                pe.wait_ge(group_out, groups_out + 1)
                pe.transpose(turn_ps[0:MAXES // 2, :, :, :].rearrange("p a b c -> p (a b c)")[:, 0:P],
                             maximum[:, par, :], ident).then_inc(max_turned, 1)

            def score(group, s, i):
                kt, j, half = i // 4, i // 2 % 2, i % 2
                pe.wait_ge(probs_ready, group * SCORES + last_reader(i))
                pe.matmul(score_ps[:, i % RING, :], k_stack[s][:, j, kt * P:(kt + 1) * P],
                          q_stack[s][:, j, half * HALF:(half + 1) * HALF], start=True, stop=True
                          ).then_inc(scores_ready, 1)

            def slot(it, s, last):
                group = it * SLOTS + s
                next_slot, next_it = (s + 1) % SLOTS, it + (s + 1) // SLOTS
                has_next = not (last and s + 1 >= SLOTS)

                def ahead(step):
                    i, later = (step + EARLY) % MAXES, (step + EARLY) // MAXES
                    if not (last and s + 1 + later >= SLOTS):
                        if i == 0:
                            pe.wait_ge(stacks_in[(s + 2) % SLOTS], (it + (s + 2) // SLOTS + 1) * STACK_DMAS * 16)
                        max_scores(group + later, (s + 1 + later) % SLOTS, i, tile_scored, tile_max)

                def mix(kt):
                    pe.wait_ge(probs_ready, group * SCORES + kt * 4 + 4 + RING)
                    if kt == 0:
                        pe.wait_ge(mixed_out, group + 1)
                        pe.wait_ge(values_in, group + 1)
                    for j in range(2):
                        for half in range(2):
                            strip = (j * 2 + half) * STRIP
                            mm = pe.matmul(mixed_ps[strip:strip + STRIP, :], values[s][:, kt, j, :],
                                           probs[:, kt % 2, j, half * HALF:(half + 1) * HALF],
                                           start=(kt == 0), stop=(kt == KEY_TILES - 1),
                                           tile_position=(0, strip))
                    mm.then_inc(probs_used, 1)

                for kt in range(1, KEY_TILES):
                    for i in range(4):
                        score(group, s, 4 * kt + i)
                        if i == 3:
                            mix(kt - 1)
                        ahead(4 * (kt - 1) + i)
                    if kt == TURN_AT and has_next:
                        turn_group_max(group + 2, (s + 1) % 2, group * 2)
                for i in range(4):
                    if i == 2:
                        mix(KEY_TILES - 1)
                    ahead(MAXES - 4 + i)
                    if has_next:
                        if i == 0:
                            pe.wait_ge(max_in[next_slot], (next_it + 1) * 16)
                        score(group + 1, next_slot, i)
                pe.wait_ge(mixed_out, group + 2)
                if has_next:
                    pe.wait_ge(max_negated, group + 2)
                else:
                    pe.wait_ge(group_out, group * 2 + 1)
                for qt in range(KEY_TILES // 2):
                    turn = pe.transpose(turn_ps[:, qt, :, :].rearrange("p a b -> p (a b)"),
                                        mixed[:, qt * P:(qt + 1) * P], ident)
                turn.then_inc(mixed_turned[s], 1)

            for s in range(SLOTS):
                pe.sem_inc(mixed_turned[s], 1)
            pe.wait_ge(stacks_in[0], STACK_DMAS * 16)
            for i in range(MAXES):
                max_scores(0, 0, i, early_scored, early_max)
            pe.wait_ge(early_max, MAXES + RING)
            pe.wait_ge(v_set, 2 * SLOTS)
            pe.wait_ge(ones_set, 2 * (SLOTS - 1))
            pe.wait_ge(stacks_in[1], STACK_DMAS * 16)
            for i in range(EARLY):
                max_scores(0, 1, i, tile_scored, tile_max)
                if i == 2:
                    turn_group_max(1, 0, 0)
            pe.wait_ge(max_in[0], 16)
            for i in range(4):
                score(0, 0, i)
            with pe.Fori(0, ITS - 1) as it:
                for s in range(SLOTS):
                    slot(it, s, False)
            for s in range(SLOTS):
                slot(ITS - 1, s, True)

        @block.scalar
        def _(act):
            def negate_maxima(count, par):
                act.wait_ge(max_turned, count)
                act.activation(max_rows[:, par, :],
                               turn_ps[0:MAXES // 2, :, :, :].rearrange("p a b c -> p (a b c)")[:, 0:P],
                               ACT.Copy, scale=-1.0).then_inc(max_negated, 1)

            def exponentials(group, indices):
                for i in indices:
                    kt, j, half = i // 4, i // 2 % 2, i % 2
                    act.wait_ge(scores_ready, group * SCORES + i + 1)
                    act.activation(probs[:, kt % 2, j, half * HALF:(half + 1) * HALF], score_ps[:, i % RING, :],
                                   ACT.Exp, scale=SCORE_SCALE).then_inc(probs_ready, 1)

            def slot(it, s, last):
                group = it * SLOTS + s
                has_next = not (last and s + 1 >= SLOTS)
                for kt in range(1, KEY_TILES):
                    if kt >= 2:
                        act.wait_ge(probs_used, group * KEY_TILES + kt - 1)
                    exponentials(group, range(4 * kt, 4 * kt + 4))
                    if kt == TURN_AT and has_next:
                        negate_maxima(group + 2, (s + 1) % 2)
                if has_next:
                    act.wait_ge(probs_used, group * KEY_TILES + KEY_TILES - 1)
                    exponentials(group + 1, (0, 1))
                act.wait_ge(probs_used, (group + 1) * KEY_TILES)
                act.activation(mixed[:, :], mixed_ps[:, :], ACT.Copy).then_inc(mixed_out, 1)
                if has_next:
                    exponentials(group + 1, (2, 3))

            for s in range(1, SLOTS):
                act.activation(q_stack[s][ROWS:P, :, :].rearrange("p j q -> p (j q)"),
                               attn["constant"][ROWS:P, 0:1].broadcast_to([P - ROWS, 2 * SEQ]), ACT.Copy, scale=0.0
                               ).then_inc(q_cleared, 1)
            act.sem_inc(mixed_out, 1)
            act.sem_inc(probs_ready, RING)
            negate_maxima(1, 0)
            exponentials(0, range(4))
            with act.Fori(0, ITS - 1) as it:
                for s in range(SLOTS):
                    slot(it, s, False)
            for s in range(SLOTS):
                slot(ITS - 1, s, True)

        @block.vector
        def _(v):
            def take_maxima(group, par, scored, taken, indices=range(MAXES)):
                for i in indices:
                    v.wait_ge(scored, group * MAXES + i + 1)
                    v.reduce_max(maxima[:, par, i // 2, i % 2:i % 2 + 1], max_ps[:, i % RING, :], axis=AXIS_X
                                 ).then_inc(taken, 1)

            def close_maxima(group, par, taken):
                v.wait_ge(taken, (group + 1) * MAXES + RING)
                v.tensor_tensor(maximum[:, par, :], maxima[:, par, :, 0], maxima[:, par, :, 1], ALU.max
                                ).then_inc(group_max, 1)

            def write_out(it, s):
                group = it * SLOTS + s
                v.wait_ge(mixed_turned[s], it + 2)
                v.reciprocal(inverse[:, :, :], turn_ps[:, :, :, HD]).then_inc(inverted, 1)
                v.wait_ge(inverted, group + 1)
                for j in range(2):
                    at = s * 2 * HD + j * HD
                    v.tensor_tensor(
                        attn["out"][:, it, :, at:at + HD].rearrange("p (half t) d -> p half t d", half=2),
                        turn_ps[:, :, 2 * j:2 * j + 2, 0:HD].rearrange("p t half d -> p half t d"),
                        inverse[:, :, 2 * j:2 * j + 2].rearrange("p t half -> p half t").unsqueeze(3)
                        .broadcast_to([P, 2, KEY_TILES // 2, HD]),
                        ALU.mult).then_inc(group_out, 1)

            def slot(it, s, last):
                group = it * SLOTS + s
                if not (last and s + 1 >= SLOTS):
                    take_maxima(group, (s + 1) % 2, tile_scored, tile_max, range(EARLY, MAXES))
                    close_maxima(group, (s + 1) % 2, tile_max)
                if not (last and s + 2 >= SLOTS):
                    take_maxima(group + 1, s % 2, tile_scored, tile_max, range(EARLY))
                if last and s == SLOTS - 2:
                    v.wait_ge(bias_in, 16)
                    v.tensor_tensor(keep["x"][:, :, :], keep["x"][:, :, :],
                                    bias_o[:, :].unsqueeze(1).broadcast_to([P, TILES, DIM]), ALU.add
                                    ).then_inc(x_biased, 1)
                write_out(it, s)

            v.sem_inc(group_out, 1)
            v.sem_inc(early_max, RING)
            v.sem_inc(tile_max, RING)
            take_maxima(0, 0, early_scored, early_max)
            close_maxima(0, 0, early_max)
            take_maxima(0, 1, tile_scored, tile_max, range(EARLY))
            with v.Fori(0, ITS - 1) as it:
                for s in range(SLOTS):
                    slot(it, s, False)
            for s in range(SLOTS):
                slot(ITS - 1, s, True)


def output_block(nc, sem, dram, keep, attn, buffers):
    x_sb, ident = keep["x"], keep["ident"]
    with ExitStack() as scope:
        def sb(n, shape, dt):
            return scope.enter_context(nc.sbuf_tensor(f"o_{n}", shape, dt))

        def psum(n, shape, dt):
            return scope.enter_context(nc.psum_tensor(f"o_{n}", shape, dt))

        stage = sb("stage", [P, KT, DIM], F32)
        w_o = sb("w", [P, KT, DIM], F32)
        lora_b, lora_a = sb("lora_b", [RANK, DIM], F32), sb("lora_a", [RANK, DIM], F32)
        rows = sb("rows", [P, 2, DIM], F32)
        columns = sb("columns", [P, 2, KT, P], F32)
        update_ps = psum("update_ps", [P, 2, DIM], F32)
        columns_ps = psum("columns_ps", [P, 2, 512], F32)
        out_ps = psum("out_ps", [P, 2, 512], F32)

        weights_in = sem("o_weights_in")
        update_ready, whole_done = sem("o_update_ready"), sem("o_whole_done")
        rows_done = sem("o_rows_done")
        turned = sem("o_turned")
        columns_done = sem("o_columns_done")
        out_ready = sem("o_out_ready")
        x_updated = sem("o_x_updated")
        block = scope.enter_context(nc.Block())

        @block.sync
        def _(sp):
            sp.dma_start(stage[:, :, :], dram["wo_t"].rearrange("(k p) o -> p k o", p=P)).then_inc(weights_in, 16)
            sp.dma_start(lora_b[:, :], dram["lora_bo"]).then_inc(weights_in, 16)
            sp.dma_start(lora_a[:, :], dram["lora_ao_t"]).then_inc(weights_in, 16)
            buffers.load(sp, dram)

        @block.tensor
        def _(pe):
            pe.sem_inc(turned, FIRST)
            pe.sem_inc(out_ready, FIRST)
            pe.wait_ge(weights_in, 48)
            for k in range(KT):
                update = pe.matmul(update_ps[:, k, :], lora_b[:, k * P:(k + 1) * P], lora_a[:, :],
                                   start=True, stop=True)
            update.then_inc(update_ready, 1)
            pe.wait_ge(whole_done, 1)

            def turn(t, par):
                pe.wait_ge(rows_done, t + 1)
                pe.wait_ge(columns_done, t + 1)
                for k in range(KT):
                    turn = pe.transpose(columns_ps[:, par, k * P:(k + 1) * P], rows[:, par, k * P:(k + 1) * P],
                                        ident[:, :])
                turn.then_inc(turned, 1)

            def product(t, par):
                pe.wait_ge(columns_done, t + 1 + FIRST)
                pe.wait_ge(x_updated, t + 1)
                for k in range(KT):
                    out = pe.matmul(out_ps[:, par, 0:DIM], columns[:, par, k, :], w_o[:, k, :],
                                    start=(k == 0), stop=(k == KT - 1))
                out.then_inc(out_ready, 1)

            turn(0, 0)
            with pe.Fori(0, TILES // 2 - 1) as pair:
                for par in range(2):
                    t = pair * 2 + par
                    turn(t + 1, 1 - par)
                    product(t, par)
            turn(TILES - 1, 1)
            product(TILES - 2, 0)
            product(TILES - 1, 1)

        @block.scalar
        def _(act):
            act.sem_inc(columns_done, FIRST)
            by_tile = attn["out"][:, :, :, :].rearrange("p (f b) j d -> p f (b j) d", f=KT)

            def gather_rows(t, par):
                act.wait_ge(turned, t + 1)
                act.activation(rows[:, par, :].rearrange("p (f d) -> p f d", f=KT), by_tile[:, :, t, :],
                               ACT.Copy).then_inc(rows_done, 1)

            def copy_columns(t, par):
                act.wait_ge(turned, t + 1 + FIRST)
                act.wait_ge(out_ready, t + 1)
                act.activation(columns[:, par, :, :].rearrange("p k q -> p (k q)"), columns_ps[:, par, 0:DIM],
                               ACT.Copy).then_inc(columns_done, 1)

            for par in range(2):
                gather_rows(par, par)
            with act.Fori(0, TILES // 2 - 1) as pair:
                for par in range(2):
                    t = pair * 2 + par
                    copy_columns(t, par)
                    gather_rows(t + 2, par)
            for par in range(2):
                copy_columns(TILES - 2 + par, par)

        @block.vector
        def _(v):
            v.sem_inc(x_updated, FIRST)
            v.wait_ge(update_ready, 1)
            v.scalar_tensor_tensor(out=w_o[:, :, :], in0=update_ps[:, :, :], scalar=LORA_SCALE,
                                   in1=stage[:, :, :], op0=ALU.mult, op1=ALU.add).then_inc(whole_done, 1)

            def update(t, par):
                v.wait_ge(out_ready, t + 1 + FIRST)
                v.tensor_tensor(x_sb[:, t, :], out_ps[:, par, 0:DIM], x_sb[:, t, :], ALU.add).then_inc(x_updated, 1)

            def statistics(t):
                v.wait_ge(x_updated, t + 1 + FIRST)
                v.bn_stats(keep["stats"][:, t, :], x_sb[:, t, :]).then_inc(keep["stats_done"], 1)

            update(0, 0)
            with v.Fori(0, TILES // 2 - 1) as pair:
                for par in range(2):
                    t = pair * 2 + par
                    update(t + 1, 1 - par)
                    statistics(t)
            update(TILES - 1, 1)
            statistics(TILES - 2)
            statistics(TILES - 1)


def attention(nc, sem, dram, keep, out, raw):
    with ExitStack() as scope:
        attn = {"ident": keep["ident"][:, :], "constant": keep["minus_half"][:, :], "out": out}
        for part in ("q_hi", "q_lo", "k_hi", "k_lo"):
            attn[part] = scope.enter_context(nc.sbuf_tensor(part, [P, KT, TOKENS], F32R))
        attn["v"] = scope.enter_context(nc.sbuf_tensor("v_rows", [P, KT, BATCH, JT, HEADS // KT, HD], F32))
        attn["stacks0"] = Stacks(nc, scope, sem, 0)
        project_block(nc, sem, dram, keep, attn, raw)
        attention_block(nc, sem, dram, keep, attn)
    return attn


def macaron(nc, dram):
    with ExitStack() as outer:
        def sb(name, shape, dt):
            return outer.enter_context(nc.sbuf_tensor(name, shape, dt))

        def sem(name):
            return outer.enter_context(nc.semaphore(name))

        keep = {
            "x": sb("x_sb", [P, TILES, DIM], F32),
            "ident": sb("ident", [P, P], F32),
            "minus_half": sb("minus_half", [P, TILES], F32),
            "route_w": sb("route_w", [P, KT, 2, 2, KEYS], F32),
            "stats": sb("stats", [P, TILES, 6], F32),
            "stats_done": sem("stats_done"),
            "ident_done": sem("ident_done"),
        }
        attn_out = sb("attn_out", [P, KT * BATCH, JT, P], F32)
        raw = RawProjections(sem, attn_out)
        with ExitStack() as scope:
            buffers = FfnBuffers(nc, scope, sem, "ffn0")
            setup_block(nc, sem, dram, keep, buffers)
            ffn_block(nc, sem, dram, keep, buffers, 0, raw)
        attn = attention(nc, sem, dram, keep, attn_out, raw)
        with ExitStack() as scope:
            buffers = FfnBuffers(nc, scope, sem, "ffn1")
            output_block(nc, sem, dram, keep, attn, buffers)
            ffn_block(nc, sem, dram, keep, buffers, 1)


def kernel(L0_attn_x, L0_attn_Wq, L0_attn_bq, L0_attn_Bq, L0_attn_Aq, L0_attn_Wk, L0_attn_bk, L0_attn_Bk,
           L0_attn_Ak, L0_attn_Wv, L0_attn_bv, L0_attn_Bv, L0_attn_Av, L0_attn_Wo, L0_attn_bo, L0_attn_Bo,
           L0_attn_Ao, L0_ffn_W_q, L0_ffn_keys, L0_ffn_down_embed, L0_ffn_up_embed, L0_ffn_gate_w,
           L0_ffn_up_w, L0_ffn_down_w):
    import numpy as np
    import concourse.bacc as bacc
    from concourse.bass_utils import run_bass_kernel_spmd

    nc = bacc.Bacc("TRN2", target_bir_lowering=False, num_devices=1)
    laid = {
        "x": np.asarray(L0_attn_x).reshape(TOKENS, DIM),
        "retrieval_t": np.asarray(L0_ffn_W_q).T, "keys": L0_ffn_keys,
        "gate": L0_ffn_gate_w, "up": L0_ffn_up_w, "down": L0_ffn_down_w,
        "down_embed": np.asarray(L0_ffn_down_embed).T, "up_embed": L0_ffn_up_embed,
    }
    for p, (w, b, bm, am) in {"q": (L0_attn_Wq, L0_attn_bq, L0_attn_Bq, L0_attn_Aq),
                              "k": (L0_attn_Wk, L0_attn_bk, L0_attn_Bk, L0_attn_Ak),
                              "v": (L0_attn_Wv, L0_attn_bv, L0_attn_Bv, L0_attn_Av),
                              "o": (L0_attn_Wo, L0_attn_bo, L0_attn_Bo, L0_attn_Ao)}.items():
        laid |= {f"w{p}_t": np.asarray(w).T, f"b{p}": b, f"lora_b{p}": bm, f"lora_a{p}_t": np.asarray(am).T}
        if p in "qk":
            laid[f"b{p}_columns"] = np.asarray(b).reshape(KT, P).T
    arrays, dram = {}, {}
    for name, a in laid.items():
        arrays[f"in_{name}"] = a = np.ascontiguousarray(a)
        dram[name] = nc.dram_tensor(f"in_{name}", a.shape, mybir.dt.from_np(a.dtype), kind="ExternalInput").ap()
    dram["out"] = nc.dram_tensor("out", (TOKENS, DIM), F32, kind="ExternalOutput").ap()
    macaron(nc, dram)
    r = run_bass_kernel_spmd(nc, [arrays], core_ids=[0])
    return np.asarray(r.results[0]["out"]).reshape(BATCH, SEQ, DIM)
```
